# Optimizing a Trainium2 kernel written in Bass

```python
import numpy as np
import jax
import jax.numpy as jnp

def _softmax(x, axis=-1):
    return jax.nn.softmax(x, axis=axis)

def _gelu(x):
    return jax.nn.gelu(x, approximate=True)

def _silu(x):
    return jax.nn.silu(x)

def _sigmoid(x):
    return jax.nn.sigmoid(x)

def _layernorm(x, axis=-1, eps=1e-05):
    m = jnp.mean(x, axis=axis, keepdims=True)
    v = jnp.var(x, axis=axis, keepdims=True)
    return (x - m) / jnp.sqrt(v + eps)

def _scatter_add(tgt, idx, src, axis=0):
    return tgt.at[idx].add(src)

def _segment_sum(src, seg, n):
    return jax.ops.segment_sum(src, seg, n)
kernel_name = 'mk_conv_seq_d2_conv_nchw512_r2_399a17'

def setup_inputs(seed: int=0):
    np.random.seed(seed)
    _w = jnp.asarray

    def _rec_inputs():
        import jax
        import jax.numpy as jnp
        _gk = jax.random.key(seed)
        x = -0.000125 + 0.9999 * jax.random.normal(jax.random.fold_in(_gk, 1), (16, 256, 32, 32), jnp.float32)
        return x
    x = _rec_inputs()

    def _L0_conv_setup():
        import jax, jax.numpy as jnp
        import numpy as np

        def _pool2(x):
            b, c, h, w = x.shape
            return x.reshape(b, c, h // 2, 2, w // 2, 2).max(axis=(3, 5))
        key = jax.random.key(seed)
        ks = jax.random.split(key, 6)
        B, C, H, W = (16, 256, 32, 32)
        x = jax.random.normal(ks[0], (B, C, H, W), dtype=jnp.float32)
        scale = 0.02
        theta_w = jax.random.normal(ks[1], (C // 8, C), dtype=jnp.float32) * scale
        phi_w = jax.random.normal(ks[2], (C // 8, C), dtype=jnp.float32) * scale
        g_w = jax.random.normal(ks[3], (C // 2, C), dtype=jnp.float32) * scale
        o_w = jax.random.normal(ks[4], (C, C // 2), dtype=jnp.float32) * scale
        gamma = jax.random.normal(ks[5], (), dtype=jnp.float32) * 0.5
        return {'x': x, 'theta_w': theta_w, 'phi_w': phi_w, 'g_w': g_w, 'o_w': o_w, 'gamma': gamma}
    _L0_conv_all = _L0_conv_setup()
    _L0_conv_in = {k: v for k, v in _L0_conv_all.items() if k in ('theta_w', 'phi_w', 'g_w', 'o_w', 'gamma')}
    del _L0_conv_all

    def _L1_conv_setup():
        import jax, jax.numpy as jnp
        import numpy as np
        SCOPE = 27
        WIDTH = 3.0
        DAMP = 0.12
        SELF_CONNECT = False

        def mexican_hat(scope, width, damp, self_connect=False):
            x = jnp.arange(scope, dtype=jnp.float32) - scope // 2
            norm = 2.0 / (np.sqrt(3.0 * width) * np.pi ** 0.25)
            w = norm * (1.0 - (x / width) ** 2) * jnp.exp(-x ** 2 / (2.0 * width ** 2))
            w = damp * w
            if not self_connect:
                w = w.at[scope // 2].set(0.0)
            return w

        def toeplitz1d_circular(filt, c):
            s = filt.shape[0]
            h = s // 2
            offsets = jnp.arange(s) - h
            rows = jnp.arange(c)[:, None]
            cols = (rows + offsets[None, :]) % c
            tpl = jnp.zeros((c, c), dtype=filt.dtype)
            tpl = tpl.at[rows, cols].set(jnp.broadcast_to(filt[None, :], (c, s)))
            return tpl
        key = jax.random.key(seed)
        k1, _ = jax.random.split(key)
        activations = jax.random.normal(k1, (32, 256, 28, 28), dtype=jnp.float32)
        inhibition_filter = mexican_hat(SCOPE, WIDTH, DAMP, self_connect=SELF_CONNECT)
        return {'activations': activations, 'inhibition_filter': inhibition_filter}
    _L1_conv_all = _L1_conv_setup()
    _L1_conv_in = {k: v for k, v in _L1_conv_all.items() if k in ('inhibition_filter',)}
    del _L1_conv_all
    return {'x': x, 'L0_conv_theta_w': _L0_conv_in['theta_w'], 'L0_conv_phi_w': _L0_conv_in['phi_w'], 'L0_conv_g_w': _L0_conv_in['g_w'], 'L0_conv_o_w': _L0_conv_in['o_w'], 'L0_conv_gamma': _L0_conv_in['gamma'], 'L1_conv_inhibition_filter': _L1_conv_in['inhibition_filter']}

def reference(x, L0_conv_theta_w, L0_conv_phi_w, L0_conv_g_w, L0_conv_o_w, L0_conv_gamma, L1_conv_inhibition_filter):
    import jax
    import jax.numpy as jnp

    def _L0_conv_ref(x, theta_w, phi_w, g_w, o_w, gamma):
        import jax, jax.numpy as jnp
        import numpy as np

        def _pool2(x):
            b, c, h, w = x.shape
            return x.reshape(b, c, h // 2, 2, w // 2, 2).max(axis=(3, 5))
        B, C, H, W = x.shape
        HW = H * W
        theta = jnp.einsum('bchw,kc->bkhw', x, theta_w).reshape(B, C // 8, HW).transpose(0, 2, 1)
        phi = _pool2(jnp.einsum('bchw,kc->bkhw', x, phi_w)).reshape(B, C // 8, HW // 4)
        beta = jax.nn.softmax(jnp.einsum('bnk,bkm->bnm', theta, phi), axis=-1)
        g = _pool2(jnp.einsum('bchw,kc->bkhw', x, g_w)).reshape(B, C // 2, HW // 4)
        o_in = jnp.einsum('bcm,bnm->bcn', g, beta).reshape(B, C // 2, H, W)
        o = jnp.einsum('bchw,kc->bkhw', o_in, o_w)
        return gamma * o + x

    def _L1_conv_ref(activations, inhibition_filter):
        import jax, jax.numpy as jnp
        import numpy as np
        SCOPE = 27
        WIDTH = 3.0
        DAMP = 0.12
        SELF_CONNECT = False

        def mexican_hat(scope, width, damp, self_connect=False):
            x = jnp.arange(scope, dtype=jnp.float32) - scope // 2
            norm = 2.0 / (np.sqrt(3.0 * width) * np.pi ** 0.25)
            w = norm * (1.0 - (x / width) ** 2) * jnp.exp(-x ** 2 / (2.0 * width ** 2))
            w = damp * w
            if not self_connect:
                w = w.at[scope // 2].set(0.0)
            return w

        def toeplitz1d_circular(filt, c):
            s = filt.shape[0]
            h = s // 2
            offsets = jnp.arange(s) - h
            rows = jnp.arange(c)[:, None]
            cols = (rows + offsets[None, :]) % c
            tpl = jnp.zeros((c, c), dtype=filt.dtype)
            tpl = tpl.at[rows, cols].set(jnp.broadcast_to(filt[None, :], (c, s)))
            return tpl
        c = activations.shape[1]
        tpl = toeplitz1d_circular(inhibition_filter, c)
        inhib = jnp.einsum('fc,bchw->bfhw', tpl, activations)
        return activations + inhib

    def _gn(v, G=32, eps=1e-05):
        B_, C_, H_, W_ = v.shape
        g = v.reshape(B_, G, C_ // G, H_, W_)
        m = jnp.mean(g, axis=(2, 3, 4), keepdims=True)
        s = jnp.var(g, axis=(2, 3, 4), keepdims=True)
        return ((g - m) / jnp.sqrt(s + eps)).reshape(v.shape)

    def _ln_c(v, eps=1e-06):
        m = jnp.mean(v, axis=1, keepdims=True)
        s = jnp.var(v, axis=1, keepdims=True)
        return (v - m) / jnp.sqrt(s + eps)

    def _ln_t(v, eps=1e-05):
        m = jnp.mean(v, axis=-1, keepdims=True)
        s = jnp.var(v, axis=-1, keepdims=True)
        return (v - m) / jnp.sqrt(s + eps)

    def _to_tokens(v):
        B_, C_, H_, W_ = v.shape
        return v.reshape(B_, C_, H_ * W_).transpose(0, 2, 1)

    def _from_tokens(t, like):
        B_, C_, H_, W_ = like.shape
        return t.transpose(0, 2, 1).reshape(B_, C_, H_, W_)
    x = _L0_conv_ref(x, L0_conv_theta_w, L0_conv_phi_w, L0_conv_g_w, L0_conv_o_w, L0_conv_gamma)
    x = _L1_conv_ref(x, L1_conv_inhibition_filter)
    return x

_drawn_inputs = setup_inputs


def setup_inputs(seed=0):
    import zlib

    import numpy as np

    out = dict(_drawn_inputs(seed))
    spreads = {}
    factors = {'L0_conv_theta_w': 8.0, 'L0_conv_phi_w': 8.0, 'L0_conv_g_w': 8.0}
    for name, (base, spread) in spreads.items():
        noise = np.random.default_rng([zlib.crc32(name.encode()), seed]).standard_normal(out[name].shape)
        drawn = base * np.exp(spread * noise) if base else spread * noise
        out[name] = jnp.asarray(drawn.astype(out[name].dtype))
    for name, factor in factors.items():
        out[name] = (out[name] * factor).astype(out[name].dtype)
    return out
```

```python
from contextlib import ExitStack

import concourse.bass as bass
from concourse import mybir

ALU = mybir.AluOpType
ACT = mybir.ActivationFunctionType
AXIS = mybir.AxisListType
F32 = mybir.dt.float32
F32R = mybir.dt.float32r

P = 128


def attention_then_channel_filter(nc, x, theta_wT, phi_wT, g_wT, o_w, gamma, taps, out, ring):
    B, C, HW = x.shape
    K = theta_wT.shape[1]
    CG = g_wT.shape[1]
    SIDE = 32
    M = HW // 4
    TAPS = taps.shape[1]
    CT = C // P
    MT = M // P
    HALF = HW // 2
    NT = HALF // P
    RH = HALF // SIDE
    MH = M // 2
    R_SHIFT = 3 * K
    K_AUG = R_SHIFT + 2
    REACH = TAPS // 2
    K_EDGE = 3 * 2 * REACH
    assert HW == SIDE * SIDE and C == 2 * P and CG == P and K == 32 and HALF == 512
    PAIRS = B // 2

    x_v = x.rearrange("b (t p) n -> b p t n", p=P)
    out_v = out.rearrange("b (t p) n -> b p t n", p=P)

    with ExitStack() as ctx:
        def sb(name, shape, dt=F32):
            return ctx.enter_context(nc.sbuf_tensor(name, shape, dt))

        def sem(name):
            return ctx.enter_context(nc.semaphore(name))

        WPROJ = 2 * CT * P
        w_raw = sb("w_raw", [P, 2, CT, P])
        w_hi = sb("w_hi", [P, 2, CT, P], F32R)
        w_lo = sb("w_lo", [P, 2, CT, P], F32R)
        o_sb = sb("o_sb", [P, CT, CG])
        gamma_sb = sb("gamma_sb", [P, 1])
        ring_sb = sb("ring_sb", [1, 2 * C])
        band_rev = sb("band_rev", [P, CT, C])
        band = sb("band", [P, CT, C])
        band_hi = sb("band_hi", [P, CT, C], F32R)
        band_lo = sb("band_lo", [P, CT, C], F32R)
        edge_w = sb("edge_w", [K_EDGE, CT * P], F32R)
        w2 = sb("w2", [P, C])
        w2_hi = sb("w2_hi", [P, C], F32R)
        w2_lo = sb("w2_lo", [P, C], F32R)
        ident = sb("ident", [P, P])
        ident_r = sb("ident_r", [P, P], F32R)

        x_raw = sb("x_raw", [P, 2, CT, HW])
        x_hi = sb("x_hi", [P, 2, CT, HW], F32R)
        x_lo = sb("x_lo", [P, 2, CT, HW], F32R)
        x_edge = sb("x_edge", [K_EDGE, 2, CT, HW], F32R)
        theta_aug = sb("theta_aug", [P, 2, HW], F32R)
        phi_aug = sb("phi_aug", [P, 2, M], F32R)
        phi_pool = sb("phi_pool", [2 * K, M])
        g_pool = sb("g_pool", [P, M])
        gT_hi = sb("gT_hi", [P, MT, CG], F32R)
        gT_lo = sb("gT_lo", [P, MT, CG], F32R)
        neg_max = sb("neg_max", [P, 2 * NT])
        exp_sum = sb("exp_sum", [P, 2 * NT])
        ln_sum = sb("ln_sum", [P, 2 * NT])
        shift = sb("shift", [P, 2 * NT])
        shift_parts = sb("shift_parts", [P, 2 * NT, 2], F32R)
        prob = sb("prob", [P, 2, MT, HALF])
        prob_hi = sb("prob_hi", [P, 2, MT, HALF], F32R)
        prob_lo = sb("prob_lo", [P, 2, MT, HALF], F32R)
        att_hi = sb("att_hi", [P, 2, HALF], F32R)
        att_lo = sb("att_lo", [P, 2, HALF], F32R)
        y = sb("y", [P, 2, CT, HW])

        psX = ctx.enter_context(nc.psum_tensor("psX", [P, 2, HALF], F32))
        psZ = ctx.enter_context(nc.psum_tensor("psZ", [P, 2, HALF], F32))
        psY = ctx.enter_context(nc.psum_tensor("psY", [P, 2, HALF], F32))
        psV = ctx.enter_context(nc.psum_tensor("psV", [P, 2, HALF], F32))
        scores_ps = [psX, psZ]
        thetaphi_ps = [psY[:, 0, :], psY[:, 1, :]]
        g_ps = [psV[:, 0, :], psY[:, 1, :]]
        att_ps = [psV[:, 1, :], psY[:, 0, :]]
        gT_ps = psY[:, 1, 0:MT * CG]
        out_ps = [[psV[:, 0, :], psV[:, 1, :]], [psY[:, 0, :], psY[:, 1, :]]]
        shift_ps = psX

        proj_w_loaded = sem("proj_w_loaded")
        o_loaded = sem("o_loaded")
        taps_loaded = sem("taps_loaded")
        ring_zeroed = sem("ring_zeroed")
        ring_ready = sem("ring_ready")
        ring_stored = sem("ring_stored")
        band_loaded = sem("band_loaded")
        band_ready = sem("band_ready")
        proj_w_hi_ready = sem("proj_w_hi_ready")
        proj_w_ready = sem("proj_w_ready")
        band_parts_ready = sem("band_parts_ready")
        edge_w_loaded = sem("edge_w_loaded")
        w2_done = sem("w2_done")
        w2_scaled = sem("w2_scaled")
        w2_parts_ready = sem("w2_parts_ready")
        ident_zeroed = sem("ident_zeroed")
        ident_ready = sem("ident_ready")
        ident_r_ready = sem("ident_r_ready")
        phi_ones_ready = sem("phi_ones_ready")

        x_loaded = [sem("x_loaded0"), sem("x_loaded1")]
        x_hi_ready = sem("x_hi_ready")
        x_lo_ready = sem("x_lo_ready")
        x_edge_loaded = [sem("x_edge_loaded0"), sem("x_edge_loaded1")]
        thetaphi_done = sem("thetaphi_done")
        theta_hi_ready = sem("theta_hi_ready")
        theta_lo_ready = sem("theta_lo_ready")
        phi_pooled = sem("phi_pooled")
        phi_hi_ready = sem("phi_hi_ready")
        phi_ready = sem("phi_ready")
        g_done = sem("g_done")
        g_pooled = sem("g_pooled")
        gT_done = sem("gT_done")
        gT_hi_ready = sem("gT_hi_ready")
        gT_lo_ready = sem("gT_lo_ready")
        scores_done = sem("scores_done")
        neg_max_ready = sem("neg_max_ready")
        exp_sum_ready = sem("exp_sum_ready")
        ln_sum_ready = sem("ln_sum_ready")
        shift_ready = sem("shift_ready")
        shift_hi_ready = sem("shift_hi_ready")
        shift_parts_ready = sem("shift_parts_ready")
        shift_rows_done = sem("shift_rows_done")
        shift_rows_ready = sem("shift_rows_ready")
        scoresT_done = sem("scoresT_done")
        prob_ready = sem("prob_ready")
        prob_hi_ready = sem("prob_hi_ready")
        prob_lo_ready = sem("prob_lo_ready")
        att_done = sem("att_done")
        att_hi_ready = sem("att_hi_ready")
        att_lo_ready = sem("att_lo_ready")
        x_used = sem("x_used")
        out_done = sem("out_done")
        out_evacuated = sem("out_evacuated")
        y_stored = [sem("y_stored0"), sem("y_stored1")]

        block = ctx.enter_context(nc.Block())

        def upto(per_image, i, par, within):
            return i * (2 * per_image) + (par * per_image + within)

        def following(i, par):
            return (i, 1) if par == 0 else (i + 1, 0)

        def over_images(engine, image):
            image(0, 0)
            image(0, 1)
            with engine.Fori(1, PAIRS - 1) as i:
                image(i, 0)
                image(i, 1)
            image(PAIRS - 1, 0)
            image(PAIRS - 1, 1)

        def is_number(i):
            return isinstance(i, int)

        def has_next(i, par):
            return not (is_number(i) and i == PAIRS - 1 and par == 1)

        def has_next_but_one(i, par):
            return not (is_number(i) and i == PAIRS - 1)

        def is_first(i, par):
            return is_number(i) and i == 0 and par == 0

        @block.sync
        def _(sp):
            def load(i, par):
                sp.dma_start(x_raw[:, par], x_v[2 * i + par]).then_inc(x_loaded[par], 16)

            load(0, 0)
            sp.dma_start(w_raw[:, 0, :, 0:K], theta_wT.rearrange("(t p) k -> p t k", p=P)).then_inc(proj_w_loaded, 16)
            sp.dma_start(w_raw[:, 0, :, K:2 * K], theta_wT.rearrange("(t p) k -> p t k", p=P)).then_inc(proj_w_loaded, 16)
            sp.dma_start(w_raw[:, 0, :, 2 * K:3 * K], phi_wT.rearrange("(t p) k -> p t k", p=P)).then_inc(proj_w_loaded, 16)
            sp.dma_start(w_raw[:, 0, :, 3 * K:], phi_wT.rearrange("(t p) k -> p t k", p=P)).then_inc(proj_w_loaded, 16)
            sp.dma_start(w_raw[:, 1], g_wT.rearrange("(t p) k -> p t k", p=P)).then_inc(proj_w_loaded, 16)
            load(0, 1)
            sp.wait_ge(ring_ready, 1)
            sp.dma_start(ring, ring_sb[0:1, :]).then_inc(ring_stored, 16)
            sp.wait_ge(ring_stored, 16)
            for t in range(CT):
                diagonals = bass.AP(tensor=ring.tensor, offset=t * P, ap=[[1, P], [1, C]])
                sp.dma_start(band_rev[:, t, :], diagonals).then_inc(band_loaded, 16)

            def stack_edges(dst, loaded, parts):
                for n, part in enumerate(parts):
                    for e, rows in enumerate((slice(0, REACH), slice(P - REACH, P))):
                        row = (2 * n + e) * REACH
                        sp.dma_start(dst[row:row + REACH].bitcast(F32), part[rows].bitcast(F32)).then_inc(loaded, 16)

            def x_edges(i, par):
                sp.wait_ge(x_lo_ready, upto(2, i, par, 2))
                stack_edges(x_edge[:, par], x_edge_loaded[par], (x_hi[:, par], x_lo[:, par], x_hi[:, par]))

            x_edges(0, 0)
            sp.wait_ge(band_parts_ready, 2)
            hi, lo = (b[:, :, :].rearrange("p t c -> p (t c)")[:, P:P + CT * P] for b in (band_hi, band_lo))
            stack_edges(edge_w[:, :], edge_w_loaded, (hi, hi, lo))

            def image(i, par):
                if has_next(i, par):
                    x_edges(*following(i, par))
                if has_next_but_one(i, par):
                    sp.wait_ge(x_hi_ready, upto(2, i, par, 2))
                    sp.wait_ge(x_lo_ready, upto(2, i, par, 2))
                    load(i + 1, par)
                sp.wait_ge(out_evacuated, upto(4, i, par, 4))
                sp.dma_start(out_v[2 * i + par], y[:, par]).then_inc(y_stored[par], 16)

            over_images(sp, image)
            sp.wait_ge(y_stored[0], 16 * PAIRS)
            sp.wait_ge(y_stored[1], 16 * PAIRS)

        @block.gpsimd
        def _(pool):
            nc.gpsimd.memset(ident[:], 0.0).then_inc(ident_zeroed, 1)
            pool.wait_ge(ident_zeroed, 1)
            nc.gpsimd.affine_select(out=ident[:], in_=ident[:], compare_op=ALU.not_equal, fill=1.0, base=0,
                                    pattern=[[-1, P]], channel_multiplier=1).then_inc(ident_ready, 1)

            def x_low(i, par, h):
                cols = slice(h * HALF, (h + 1) * HALF)
                pool.wait_ge(x_hi_ready, upto(2, i, par, h + 1))
                nc.gpsimd.tensor_tensor(x_lo[:, par, :, cols], x_raw[:, par, :, cols],
                                        x_hi[:, par, :, cols].bitcast(F32), ALU.subtract).then_inc(x_lo_ready, 1)

            for par in range(2):
                for h in range(2):
                    x_low(0, par, h)

            def image(i, par):
                if has_next_but_one(i, par):
                    for h in range(2):
                        x_low(i + 1, par, h)

            over_images(pool, image)

        @block.scalar
        def _(act):
            nc.scalar.preload_act_table_set("natural_log_exp_and_others")
            act.dma_start(o_sb[:], o_w.rearrange("(t p) k -> p t k", p=P)).then_inc(o_loaded, 16)
            act.dma_start(gamma_sb[:], gamma.partition_broadcast(P)).then_inc(o_loaded, 16)
            act.wait_ge(ring_zeroed, 1)
            mid = C - 1 - TAPS // 2
            wrap = TAPS // 2
            act.dma_start(ring_sb[0:1, mid:mid + TAPS], taps).then_inc(taps_loaded, 16)
            act.dma_start(ring_sb[0:1, 0:wrap], taps[:, TAPS - wrap:]).then_inc(taps_loaded, 16)
            act.dma_start(ring_sb[0:1, mid + C:2 * C - 1], taps[:, 0:2 * C - 1 - mid - C]).then_inc(taps_loaded, 16)

            def x_high(i, par, h):
                cols = slice(h * HALF, (h + 1) * HALF)
                if h == 0:
                    act.wait_ge(x_loaded[par], 16 * (i + 1))
                if not is_number(i) or i > 0:
                    act.wait_ge(x_used, upto(2, i, par, h - 3))
                nc.scalar.copy(x_hi[:, par, :, cols], x_raw[:, par, :, cols]).then_inc(x_hi_ready, 1)

            def theta_high(i, par, h):
                act.wait_ge(thetaphi_done, upto(2, i, par, h + 1))
                nc.scalar.copy(theta_aug[0:2 * K, par, h * HALF:(h + 1) * HALF],
                               thetaphi_ps[h][0:2 * K, :]).then_inc(theta_hi_ready, 1)

            def exp_sums(i, par, h):
                act.wait_ge(neg_max_ready, upto(2, i, par, h + 1))
                tiles = scores_ps[h][:, :, :].rearrange("p a (b m) -> p (a b) m", m=M)
                for t in range(NT):
                    col = h * NT + t
                    last = nc.scalar.activation(tiles[:, t, :], tiles[:, t, :], ACT.Exp,
                                                bias=neg_max[:, col:col + 1], accum_out=exp_sum[:, col:col + 1])
                last.then_inc(exp_sum_ready, 1)

            def ln_sums(i, par):
                act.wait_ge(exp_sum_ready, upto(2, i, par, 2))
                nc.scalar.activation(ln_sum[:], exp_sum[:], ACT.Ln).then_inc(ln_sum_ready, 1)

            def gT_high(i, par):
                act.wait_ge(gT_done, upto(1, i, par, 1))
                nc.scalar.copy(gT_hi[:, :, :], gT_ps.rearrange("p (t c) -> p t c", t=MT)).then_inc(gT_hi_ready, 1)

            def probabilities(i, par, h):
                act.wait_ge(scoresT_done, upto(2, i, par, h + 1))
                nc.scalar.activation(prob[:, h], scores_ps[h][:, :, :], ACT.Exp).then_inc(prob_ready, 1)

            def att_high(i, par, h):
                act.wait_ge(att_done, upto(2, i, par, h + 1))
                nc.scalar.copy(att_hi[:, h, :], att_ps[h]).then_inc(att_hi_ready, 1)

            def out_of_psum(i, par, h, f):
                act.wait_ge(out_done, upto(4, i, par, 2 * h + f + 1))
                nc.scalar.copy(y[:, par, f, h * HALF:(h + 1) * HALF], out_ps[h][f]).then_inc(out_evacuated, 1)

            for h in range(2):
                x_high(0, 0, h)
            for h in range(2):
                theta_high(0, 0, h)
            for h in range(2):
                x_high(0, 1, h)
            for h in range(2):
                exp_sums(0, 0, h)
            ln_sums(0, 0)
            gT_high(0, 0)

            def image(i, par):
                ni, npar = following(i, par)
                ahead = has_next(i, par)
                probabilities(i, par, 0)
                if ahead:
                    theta_high(ni, npar, 0)
                probabilities(i, par, 1)
                if ahead:
                    theta_high(ni, npar, 1)
                att_high(i, par, 0)
                if ahead:
                    exp_sums(ni, npar, 0)
                att_high(i, par, 1)
                if ahead:
                    exp_sums(ni, npar, 1)
                    ln_sums(ni, npar)
                if has_next_but_one(i, par):
                    x_high(i + 1, par, 0)
                if not (is_number(i) and i == 0):
                    act.wait_ge(y_stored[par], 16 * i)
                for f in range(CT):
                    out_of_psum(i, par, 0, f)
                if ahead:
                    gT_high(ni, npar)
                if has_next_but_one(i, par):
                    x_high(i + 1, par, 1)
                for f in range(CT):
                    out_of_psum(i, par, 1, f)

            over_images(act, image)

        @block.vector
        def _(dve):
            nc.vector.memset(ring_sb[:], 0.0).then_inc(ring_zeroed, 1)
            nc.vector.memset(phi_aug[R_SHIFT:P, :, :].bitcast(F32), 1.0).then_inc(phi_ones_ready, 1)
            dve.wait_ge(ident_ready, 1)
            nc.vector.tensor_copy(ident_r[:], ident[:]).then_inc(ident_r_ready, 1)
            dve.wait_ge(proj_w_loaded, 5 * 16)
            nc.vector.tensor_copy(w_hi[:], w_raw[:]).then_inc(proj_w_hi_ready, 1)
            dve.wait_ge(proj_w_hi_ready, 1)
            nc.vector.tensor_tensor(w_lo[:], w_raw[:], w_hi[:].bitcast(F32), ALU.subtract).then_inc(proj_w_ready, 1)
            dve.wait_ge(taps_loaded, 3 * 16)
            nc.vector.tensor_scalar_add(ring_sb[0:1, C - 1:C], ring_sb[0:1, C - 1:C], 1.0).then_inc(ring_ready, 1)

            def band_and_w2():
                dve.wait_ge(band_loaded, CT * 16)
                nc.vector.tensor_copy(band[:], band_rev[:, :, ::-1]).then_inc(band_ready, 1)
                dve.wait_ge(band_ready, 1)
                nc.vector.tensor_copy(band_hi[:], band[:]).then_inc(band_parts_ready, 1)
                dve.wait_ge(band_parts_ready, 1)
                nc.vector.tensor_tensor(band_lo[:], band[:], band_hi[:].bitcast(F32),
                                        ALU.subtract).then_inc(band_parts_ready, 1)
                dve.wait_ge(w2_done, 1)
                dve.wait_ge(o_loaded, 2 * 16)
                nc.vector.tensor_scalar(w2[:], psV[:, 0, 0:C], gamma_sb[:, 0:1], None, ALU.mult).then_inc(w2_scaled, 1)
                dve.wait_ge(w2_scaled, 1)
                nc.vector.tensor_copy(w2_hi[:], w2[:]).then_inc(w2_parts_ready, 1)
                dve.wait_ge(w2_parts_ready, 1)
                nc.vector.tensor_tensor(w2_lo[:], w2[:], w2_hi[:].bitcast(F32), ALU.subtract).then_inc(w2_parts_ready, 1)

            def pool2(dst, src):
                nonlocal_view = src.rearrange("p (r a c b) -> p r c a b", a=2, b=2, c=SIDE // 2)
                return nc.vector.tensor_reduce(dst.rearrange("p (r c) -> p r c", c=SIDE // 2), nonlocal_view,
                                               AXIS.XY, ALU.max)

            def theta_low(i, par, h):
                cols = slice(h * HALF, (h + 1) * HALF)
                dve.wait_ge(theta_hi_ready, upto(2, i, par, h + 1))
                nc.vector.tensor_tensor(theta_aug[2 * K:3 * K, par, cols], thetaphi_ps[h][0:K, :],
                                        theta_aug[0:K, par, cols].bitcast(F32), ALU.subtract).then_inc(theta_lo_ready, 1)

            def pool_phi(i, par, h):
                dve.wait_ge(thetaphi_done, upto(2, i, par, h + 1))
                pool2(phi_pool[:, h * MH:(h + 1) * MH], thetaphi_ps[h][2 * K:4 * K, :]).then_inc(phi_pooled, 1)

            def split_phi(i, par):
                dve.wait_ge(phi_pooled, upto(2, i, par, 2))
                nc.vector.tensor_copy(phi_aug[2 * K:3 * K, par, :], phi_pool[0:K, :])
                nc.vector.tensor_copy(phi_aug[0:2 * K, par, :], phi_pool[:, :]).then_inc(phi_hi_ready, 1)
                dve.wait_ge(phi_hi_ready, upto(1, i, par, 1))
                nc.vector.tensor_tensor(phi_aug[K:2 * K, par, :], phi_pool[K:2 * K, :],
                                        phi_aug[K:2 * K, par, :].bitcast(F32), ALU.subtract).then_inc(phi_ready, 1)

            def pool_g(i, par, h):
                dve.wait_ge(g_done, upto(2, i, par, h + 1))
                pool2(g_pool[:, h * MH:(h + 1) * MH], g_ps[h]).then_inc(g_pooled, 1)

            def gT_low(i, par):
                dve.wait_ge(gT_hi_ready, upto(1, i, par, 1))
                nc.vector.tensor_tensor(gT_lo[:, :, :], gT_ps.rearrange("p (t c) -> p t c", t=MT),
                                        gT_hi[:, :, :].bitcast(F32), ALU.subtract).then_inc(gT_lo_ready, 1)

            def maxima(i, par, h):
                dve.wait_ge(scores_done, upto(2, i, par, h + 1))
                tiles = scores_ps[h][:, :, :].rearrange("p a (b m) -> p (a b) m", m=M)
                nc.vector.tensor_reduce(neg_max[:, h * NT:(h + 1) * NT], tiles, AXIS.X, ALU.max,
                                        negate=True).then_inc(neg_max_ready, 1)

            def shifts(i, par):
                dve.wait_ge(ln_sum_ready, upto(1, i, par, 1))
                nc.vector.tensor_tensor(shift[:], neg_max[:], ln_sum[:], ALU.subtract).then_inc(shift_ready, 1)
                dve.wait_ge(shift_ready, upto(1, i, par, 1))
                nc.vector.tensor_copy(shift_parts[:, :, 0], shift[:]).then_inc(shift_hi_ready, 1)
                dve.wait_ge(shift_hi_ready, upto(1, i, par, 1))
                nc.vector.tensor_tensor(shift_parts[:, :, 1], shift[:], shift_parts[:, :, 0].bitcast(F32),
                                        ALU.subtract).then_inc(shift_parts_ready, 1)

            def shift_rows(i, par):
                dve.wait_ge(shift_rows_done, upto(1, i, par, 1))
                nc.vector.tensor_copy(theta_aug[R_SHIFT:K_AUG, par, :],
                                      shift_ps[0:2, :, :].rearrange("p a n -> p (a n)")).then_inc(shift_rows_ready, 1)

            def split_prob(i, par, h):
                dve.wait_ge(prob_ready, upto(2, i, par, h + 1))
                nc.vector.tensor_copy(prob_hi[:, h], prob[:, h]).then_inc(prob_hi_ready, 1)
                dve.wait_ge(prob_hi_ready, upto(2, i, par, h + 1))
                nc.vector.tensor_tensor(prob_lo[:, h], prob[:, h], prob_hi[:, h].bitcast(F32),
                                        ALU.subtract).then_inc(prob_lo_ready, 1)

            def att_low(i, par, h):
                dve.wait_ge(att_hi_ready, upto(2, i, par, h + 1))
                nc.vector.tensor_tensor(att_lo[:, h, :], att_ps[h], att_hi[:, h, :].bitcast(F32),
                                        ALU.subtract).then_inc(att_lo_ready, 1)

            for h in range(2):
                pool_phi(0, 0, h)
                theta_low(0, 0, h)
            split_phi(0, 0)
            for h in range(2):
                pool_g(0, 0, h)
            for h in range(2):
                maxima(0, 0, h)
            gT_low(0, 0)
            shifts(0, 0)
            shift_rows(0, 0)
            band_and_w2()

            def image(i, par):
                ni, npar = following(i, par)
                ahead = has_next(i, par)
                split_prob(i, par, 0)
                if ahead:
                    for h in range(2):
                        pool_phi(ni, npar, h)
                        theta_low(ni, npar, h)
                    split_phi(ni, npar)
                split_prob(i, par, 1)
                if ahead:
                    pool_g(ni, npar, 0)
                    maxima(ni, npar, 0)
                att_low(i, par, 0)
                if ahead:
                    maxima(ni, npar, 1)
                    pool_g(ni, npar, 1)
                att_low(i, par, 1)
                if ahead:
                    shifts(ni, npar)
                    gT_low(ni, npar)
                    shift_rows(ni, npar)

            over_images(dve, image)

        @block.tensor
        def _(pe):
            def three(dst, w_parts, v_parts, first, last):
                (wh, wl), (vh, vl) = w_parts, v_parts
                nc.tensor.matmul(dst, wh, vh, start=first, stop=False)
                nc.tensor.matmul(dst, wh, vl, start=False, stop=False)
                return nc.tensor.matmul(dst, wl, vh, start=False, stop=last)

            def x_parts(par, t, h):
                cols = slice(h * HALF, (h + 1) * HALF)
                return x_hi[:, par, t, cols], x_lo[:, par, t, cols]

            def project(kind, dst, i, par, h, done):
                pe.wait_ge(x_lo_ready, upto(2, i, par, h + 1))
                for t in range(CT):
                    last = three(dst, (w_hi[:, kind, t, :], w_lo[:, kind, t, :]), x_parts(par, t, h),
                                 t == 0, t == CT - 1)
                last.then_inc(done, 1)

            def theta_phi(i, par, h):
                if not is_number(i) or i > 0:
                    pe.wait_ge(out_evacuated, upto(4, i, par, h - 5))
                project(0, thetaphi_ps[h], i, par, h, thetaphi_done)

            def g_projection(i, par, h):
                if h == 0 and (not is_number(i) or i > 0):
                    pe.wait_ge(out_evacuated, upto(4, i, par, -7))
                if h == 1:
                    pe.wait_ge(theta_lo_ready, upto(2, i, par, 2))
                    pe.wait_ge(phi_pooled, upto(2, i, par, 2))
                project(1, g_ps[h], i, par, h, g_done)

            def transpose_g(i, par):
                pe.wait_ge(g_pooled, upto(2, i, par, 2))
                for t in range(MT):
                    last = nc.tensor.transpose(gT_ps[:, t * CG:(t + 1) * CG], g_pool[:, t * P:(t + 1) * P], ident[:])
                last.then_inc(gT_done, 1)

            def scores(i, par, h):
                pe.wait_ge(theta_lo_ready, upto(2, i, par, h + 1))
                pe.wait_ge(phi_ready, upto(1, i, par, 1))
                if not is_first(i, par):
                    pe.wait_ge(prob_ready, upto(2, i, par, h - 1))
                tiles = scores_ps[h][:, :, :].rearrange("p a (b m) -> p (a b) m", m=M)
                for t in range(NT):
                    n0 = h * HALF + t * P
                    last = nc.tensor.matmul(tiles[:, t, :], theta_aug[0:R_SHIFT, par, n0:n0 + P],
                                            phi_aug[0:R_SHIFT, par, :], start=True, stop=True)
                last.then_inc(scores_done, 1)

            def shifts_to_rows(i, par):
                pe.wait_ge(shift_parts_ready, upto(1, i, par, 1))
                for t in range(2 * NT):
                    last = nc.tensor.matmul(shift_ps[0:2, t // NT, (t % NT) * P:(t % NT + 1) * P],
                                            shift_parts[:, t, :], ident_r[:], start=True, stop=True)
                last.then_inc(shift_rows_done, 1)

            def scores_transposed(i, par, h):
                pe.wait_ge(shift_rows_ready, upto(1, i, par, 1))
                for t in range(MT):
                    last = nc.tensor.matmul(scores_ps[h][:, t, :], phi_aug[0:K_AUG, par, t * P:(t + 1) * P],
                                            theta_aug[0:K_AUG, par, h * HALF:(h + 1) * HALF], start=True, stop=True)
                last.then_inc(scoresT_done, 1)

            def attend(i, par, h):
                if h == 0:
                    pe.wait_ge(gT_lo_ready, upto(1, i, par, 1))
                    if not is_first(i, par):
                        pe.wait_ge(out_evacuated, upto(4, i, par, -2))
                else:
                    if has_next(i, par):
                        ni, npar = following(i, par)
                        pe.wait_ge(theta_lo_ready, upto(2, ni, npar, 1))
                        pe.wait_ge(phi_pooled, upto(2, ni, npar, 1))
                    else:
                        pe.wait_ge(out_evacuated, upto(4, i, par, -1))
                pe.wait_ge(prob_lo_ready, upto(2, i, par, h + 1))
                for t in range(MT):
                    last = three(att_ps[h], (gT_hi[:, t, :], gT_lo[:, t, :]), (prob_hi[:, h, t, :], prob_lo[:, h, t, :]),
                                 t == 0, t == MT - 1)
                last.then_inc(att_done, 1)

            def filter_x(i, par, h, f):
                if is_first(i, par) and h == 0 and f == 0:
                    pe.wait_ge(band_parts_ready, 2)
                    pe.wait_ge(edge_w_loaded, 6 * 16)
                cols = slice(f * P, (f + 1) * P)
                three(out_ps[h][f], (band_hi[:, f, cols], band_lo[:, f, cols]), x_parts(par, f, h), True, False)
                if h == 0 and f == 0:
                    pe.wait_ge(x_edge_loaded[par], 6 * 16 * (i + 1))
                other = 1 - f
                last = nc.tensor.matmul(out_ps[h][f], edge_w[:, other * P:(other + 1) * P],
                                        x_edge[:, par, other, h * HALF:(h + 1) * HALF], start=False, stop=False)
                if f == CT - 1:
                    last.then_inc(x_used, 1)

            def add_attention(i, par, h, f):
                pe.wait_ge(att_lo_ready, upto(2, i, par, h + 1))
                cols = slice(f * P, (f + 1) * P)
                three(out_ps[h][f], (w2_hi[:, cols], w2_lo[:, cols]), (att_hi[:, h, :], att_lo[:, h, :]),
                      False, True).then_inc(out_done, 1)

            pe.wait_ge(proj_w_ready, 1)
            for h in range(2):
                theta_phi(0, 0, h)
            g_projection(0, 0, 0)
            pe.wait_ge(phi_ones_ready, 1)
            for h in range(2):
                scores(0, 0, h)
            g_projection(0, 0, 1)
            pe.wait_ge(ident_ready, 1)
            transpose_g(0, 0)
            pe.wait_ge(ident_r_ready, 1)
            shifts_to_rows(0, 0)
            pe.wait_ge(o_loaded, 2 * 16)
            pe.wait_ge(band_ready, 1)
            for t in range(CT):
                last = nc.tensor.matmul(psV[:, 0, 0:C], o_sb[:, t, :], band[:, t, :], start=t == 0, stop=t == CT - 1)
            last.then_inc(w2_done, 1)
            pe.wait_ge(w2_parts_ready, 2)

            def image(i, par):
                ni, npar = following(i, par)
                ahead = has_next(i, par)
                scores_transposed(i, par, 0)
                if ahead:
                    theta_phi(ni, npar, 0)
                scores_transposed(i, par, 1)
                if ahead:
                    theta_phi(ni, npar, 1)
                    g_projection(ni, npar, 0)
                attend(i, par, 0)
                if ahead:
                    scores(ni, npar, 0)
                attend(i, par, 1)
                if ahead:
                    scores(ni, npar, 1)
                    g_projection(ni, npar, 1)
                if ahead:
                    pe.wait_ge(g_pooled, upto(2, ni, npar, 1))
                filter_x(i, par, 0, 0)
                pe.wait_ge(att_lo_ready, upto(2, i, par, 1))
                filter_x(i, par, 0, 1)
                for f in range(CT):
                    add_attention(i, par, 0, f)
                if ahead:
                    transpose_g(ni, npar)
                pe.wait_ge(att_lo_ready, upto(2, i, par, 2))
                filter_x(i, par, 1, 0)
                if ahead:
                    shifts_to_rows(ni, npar)
                    pe.wait_ge(gT_lo_ready, upto(1, ni, npar, 1))
                filter_x(i, par, 1, 1)
                for f in range(CT):
                    add_attention(i, par, 1, f)

            over_images(pe, image)


def kernel(x, L0_conv_theta_w, L0_conv_phi_w, L0_conv_g_w, L0_conv_o_w, L0_conv_gamma, L1_conv_inhibition_filter):
    import numpy as np
    import concourse.bacc as bacc
    from concourse.bass_utils import run_bass_kernel_spmd

    x = np.asarray(x)
    B, C, H, W = x.shape
    arrays = {
        "x": np.ascontiguousarray(x).reshape(B, C, H * W),
        "theta_wT": np.ascontiguousarray(np.asarray(L0_conv_theta_w).T),
        "phi_wT": np.ascontiguousarray(np.asarray(L0_conv_phi_w).T),
        "g_wT": np.ascontiguousarray(np.asarray(L0_conv_g_w).T),
        "o_w": np.ascontiguousarray(np.asarray(L0_conv_o_w)),
        "gamma": np.asarray(L0_conv_gamma).reshape(1),
        "taps": np.asarray(L1_conv_inhibition_filter).reshape(1, -1),
    }
    nc = bacc.Bacc("TRN2", target_bir_lowering=False, num_devices=1)
    aps = [nc.dram_tensor(name, a.shape, mybir.dt.from_np(a.dtype), kind="ExternalInput").ap()
           for name, a in arrays.items()]
    out = nc.dram_tensor("out", (B, C, H * W), F32, kind="ExternalOutput").ap()
    ring = nc.dram_tensor("ring", (1, 2 * C), F32, kind="Internal").ap()
    attention_then_channel_filter(nc, *aps, out, ring)
    got = run_bass_kernel_spmd(nc, [arrays], core_ids=[0])
    return got.results[0]["out"].reshape(B, C, H, W)
```

```python
from contextlib import ExitStack

import concourse.bass as bass
from concourse import mybir

ALU = mybir.AluOpType
ACT = mybir.ActivationFunctionType
AXIS = mybir.AxisListType
F32 = mybir.dt.float32
F32R = mybir.dt.float32r

P = 128


def attention_then_channel_filter(nc, x, theta_wT, phi_wT, g_wT, o_w, gamma, taps, out, ring):
    B, C, HW = x.shape
    K = theta_wT.shape[1]
    CG = g_wT.shape[1]
    SIDE = 32
    M = HW // 4
    TAPS = taps.shape[1]
    CT = C // P
    MT = M // P
    HALF = HW // 2
    NT = HALF // P
    RH = HALF // SIDE
    MH = M // 2
    R_SHIFT = 3 * K
    SHIFT_ROWS = 2 * 2 * NT
    K_AUG = R_SHIFT + SHIFT_ROWS
    REACH = TAPS // 2
    K_EDGE = 3 * 2 * REACH
    assert HW == SIDE * SIDE and C == 2 * P and CG == P and K == 32 and HALF == 512
    PAIRS = B // 2

    x_v = x.rearrange("b (t p) n -> b p t n", p=P)
    out_v = out.rearrange("b (t p) n -> b p t n", p=P)

    with ExitStack() as ctx:
        def sb(name, shape, dt=F32):
            return ctx.enter_context(nc.sbuf_tensor(name, shape, dt))

        def sem(name):
            return ctx.enter_context(nc.semaphore(name))

        tp_raw = sb("tp_raw", [P, CT, 2, K])
        g_raw = sb("g_raw", [P, CT, P])
        w_hi = sb("w_hi", [P, 2, CT, P], F32R)
        w_lo = sb("w_lo", [P, 2, CT, P], F32R)
        o_sb = sb("o_sb", [P, CT, CG])
        gamma_sb = sb("gamma_sb", [P, 1])
        taps_sb = sb("taps_sb", [1, TAPS])
        ring_sb = sb("ring_sb", [1, 2 * C])
        band_rev = sb("band_rev", [P, CT, C])
        band = sb("band", [P, CT, C])
        band_hi = sb("band_hi", [P, CT, C], F32R)
        band_lo = sb("band_lo", [P, CT, C], F32R)
        edge_w = sb("edge_w", [K_EDGE, CT * P], F32R)
        w2 = sb("w2", [P, C])
        w2_hi = sb("w2_hi", [P, C], F32R)
        w2_lo = sb("w2_lo", [P, C], F32R)
        ident = sb("ident", [P, P])
        own_tile = sb("own_tile", [SHIFT_ROWS, 2 * NT, P])
        ident_r = sb("ident_r", [P, P], F32R)

        x_raw = sb("x_raw", [P, 2, CT, HW])
        x_hi = sb("x_hi", [P, 2, CT, HW], F32R)
        x_lo = sb("x_lo", [P, 2, CT, HW], F32R)
        x_edge = sb("x_edge", [K_EDGE, 2, CT, HW], F32R)
        theta_aug = sb("theta_aug", [P, 2, HW], F32R)
        phi_aug = sb("phi_aug", [P, 2, M], F32R)
        phi_pool = sb("phi_pool", [2 * K, M])
        g_pool = sb("g_pool", [P, M])
        gT_hi = sb("gT_hi", [P, MT, CG], F32R)
        gT_lo = sb("gT_lo", [P, MT, CG], F32R)
        neg_max = sb("neg_max", [P, 2 * NT])
        exp_sum = sb("exp_sum", [P, 2 * NT])
        ln_sum = sb("ln_sum", [P, 2 * NT])
        shift = sb("shift", [P, 2 * NT])
        shift_parts = sb("shift_parts", [P, 2 * NT, 2], F32R)
        prob = sb("prob", [P, 2, MT, HALF])
        prob_hi = sb("prob_hi", [P, 2, MT, HALF], F32R)
        prob_lo = sb("prob_lo", [P, 2, MT, HALF], F32R)
        att_hi = sb("att_hi", [P, 2, HALF], F32R)
        att_lo = sb("att_lo", [P, 2, HALF], F32R)
        y = sb("y", [P, 2, CT, HW])

        psX = ctx.enter_context(nc.psum_tensor("psX", [P, 2, HALF], F32))
        psZ = ctx.enter_context(nc.psum_tensor("psZ", [P, 2, HALF], F32))
        psY = ctx.enter_context(nc.psum_tensor("psY", [P, 2, HALF], F32))
        psV = ctx.enter_context(nc.psum_tensor("psV", [P, 2, HALF], F32))
        scores_ps = [psX, psZ]
        thetaphi_ps = [psY[:, 0, :], psY[:, 1, :]]
        g_ps = [psV[:, 0, :], psY[:, 1, :]]
        att_ps = [psV[:, 1, :], psY[:, 0, :]]
        gT_ps = psY[:, 1, 0:MT * CG]
        out_ps = [[psV[:, 0, :], psV[:, 1, :]], [psY[:, 0, :], psY[:, 1, :]]]
        w2_ps = psV[:, 1, 0:C]
        shift_ps = psZ[0:SHIFT_ROWS, 0, 0:P]

        proj_w_loaded = sem("proj_w_loaded")
        g_w_loaded = sem("g_w_loaded")
        g_w_hi_ready = sem("g_w_hi_ready")
        g_w_ready = sem("g_w_ready")
        o_loaded = sem("o_loaded")
        taps_loaded = sem("taps_loaded")
        ring_zeroed = sem("ring_zeroed")
        ring_filled = sem("ring_filled")
        ring_ready = sem("ring_ready")
        ring_stored = sem("ring_stored")
        band_loaded = sem("band_loaded")
        band_ready = sem("band_ready")
        proj_w_hi_ready = sem("proj_w_hi_ready")
        proj_w_ready = sem("proj_w_ready")
        band_parts_ready = sem("band_parts_ready")
        edge_w_loaded = sem("edge_w_loaded")
        w2_done = sem("w2_done")
        w2_scaled = sem("w2_scaled")
        w2_parts_ready = sem("w2_parts_ready")
        ident_zeroed = sem("ident_zeroed")
        ident_ready = sem("ident_ready")
        ident_r_ready = sem("ident_r_ready")
        own_tile_ready = sem("own_tile_ready")
        phi_ones_ready = sem("phi_ones_ready")

        x0_loaded = [sem("x0_loaded0"), sem("x0_loaded1")]
        x_loaded = [sem("x_loaded0"), sem("x_loaded1")]
        x_hi_ready = [sem("x_hi_ready0"), sem("x_hi_ready1")]
        x_lo_ready = sem("x_lo_ready")
        x_edge_loaded = [sem("x_edge_loaded0"), sem("x_edge_loaded1")]
        thetaphi_done = sem("thetaphi_done")
        theta_hi_ready = sem("theta_hi_ready")
        theta_lo_ready = sem("theta_lo_ready")
        phi_pooled = sem("phi_pooled")
        phi_hi_ready = sem("phi_hi_ready")
        phi_ready = sem("phi_ready")
        g_done = sem("g_done")
        g_pooled = sem("g_pooled")
        gT_done = sem("gT_done")
        gT_hi_ready = sem("gT_hi_ready")
        gT_lo_ready = sem("gT_lo_ready")
        scores_done = sem("scores_done")
        neg_max_ready = sem("neg_max_ready")
        exp_sum_ready = sem("exp_sum_ready")
        ln_sum_ready = sem("ln_sum_ready")
        shift_ready = sem("shift_ready")
        shift_hi_ready = sem("shift_hi_ready")
        shift_parts_ready = sem("shift_parts_ready")
        shift_rows_done = sem("shift_rows_done")
        shift_rows_ready = sem("shift_rows_ready")
        scoresT_done = sem("scoresT_done")
        prob_ready = sem("prob_ready")
        prob_hi_ready = sem("prob_hi_ready")
        prob_lo_ready = sem("prob_lo_ready")
        att_done = sem("att_done")
        att_hi_ready = sem("att_hi_ready")
        att_lo_ready = sem("att_lo_ready")
        x_used = sem("x_used")
        out_done = sem("out_done")
        out_evacuated = sem("out_evacuated")
        y_stored = [sem("y_stored0"), sem("y_stored1")]

        block = ctx.enter_context(nc.Block())

        def upto(per_image, i, par, within):
            return i * (2 * per_image) + (par * per_image + within)

        def following(i, par):
            return (i, 1) if par == 0 else (i + 1, 0)

        def over_images(engine, image):
            image(0, 0)
            image(0, 1)
            with engine.Fori(1, PAIRS - 1) as i:
                image(i, 0)
                image(i, 1)
            image(PAIRS - 1, 0)
            image(PAIRS - 1, 1)

        def is_number(i):
            return isinstance(i, int)

        def has_next(i, par):
            return not (is_number(i) and i == PAIRS - 1 and par == 1)

        def has_next_but_one(i, par):
            return not (is_number(i) and i == PAIRS - 1)

        def is_first(i, par):
            return is_number(i) and i == 0 and par == 0

        @block.sync
        def _(sp):
            def load(i, par):
                sp.dma_start(x_raw[:, par], x_v[2 * i + par]).then_inc(x_loaded[par], 16)

            sp.dma_start(tp_raw[:, :, 0, :], theta_wT.rearrange("(t p) k -> p t k", p=P)).then_inc(proj_w_loaded, 16)
            sp.dma_start(tp_raw[:, :, 1, :], phi_wT.rearrange("(t p) k -> p t k", p=P)).then_inc(proj_w_loaded, 16)
            for h in range(2):
                cols = slice(h * HALF, (h + 1) * HALF)
                sp.dma_start(x_raw[:, 0, :, cols], x_v[0][:, :, cols]).then_inc(x0_loaded[h], 16)
            sp.dma_start(g_raw[:], g_wT.rearrange("(t p) k -> p t k", p=P)).then_inc(g_w_loaded, 16)
            sp.wait_ge(ring_ready, 1)
            sp.dma_start(ring, ring_sb[0:1, :]).then_inc(ring_stored, 16)
            sp.wait_ge(ring_stored, 16)
            for t in range(CT):
                diagonals = bass.AP(tensor=ring.tensor, offset=t * P, ap=[[1, P], [1, C]])
                sp.dma_start(band_rev[:, t, :], diagonals).then_inc(band_loaded, 16)
            load(0, 1)

            def stack_edges(dst, loaded, parts):
                for n, part in enumerate(parts):
                    for e, rows in enumerate((slice(0, REACH), slice(P - REACH, P))):
                        row = (2 * n + e) * REACH
                        sp.dma_start(dst[row:row + REACH].bitcast(F32), part[rows].bitcast(F32)).then_inc(loaded, 16)

            def x_edges(i, par):
                sp.wait_ge(x_lo_ready, upto(2, i, par, 2))
                stack_edges(x_edge[:, par], x_edge_loaded[par], (x_hi[:, par], x_lo[:, par], x_hi[:, par]))

            sp.wait_ge(band_parts_ready, 2)
            hi, lo = (b[:, :, :].rearrange("p t c -> p (t c)")[:, P:P + CT * P] for b in (band_hi, band_lo))
            stack_edges(edge_w[:, :], edge_w_loaded, (hi, hi, lo))
            x_edges(0, 0)

            def image(i, par):
                if has_next(i, par):
                    x_edges(*following(i, par))
                if has_next_but_one(i, par):
                    sp.wait_ge(x_lo_ready, upto(2, i, par, 2))
                    load(i + 1, par)
                sp.wait_ge(out_evacuated, upto(4, i, par, 4))
                sp.dma_start(out_v[2 * i + par], y[:, par]).then_inc(y_stored[par], 16)

            over_images(sp, image)
            sp.wait_ge(y_stored[0], 16 * PAIRS)
            sp.wait_ge(y_stored[1], 16 * PAIRS)

        @block.gpsimd
        def _(pool):
            pool.dma_start(o_sb[:], o_w.rearrange("(t p) k -> p t k", p=P)).then_inc(o_loaded, 16)
            pool.dma_start(gamma_sb[:], gamma.partition_broadcast(P)).then_inc(o_loaded, 16)
            nc.gpsimd.memset(ident[:], 0.0).then_inc(ident_zeroed, 1)
            pool.wait_ge(ident_zeroed, 1)
            nc.gpsimd.affine_select(out=ident[:], in_=ident[:], compare_op=ALU.not_equal, fill=1.0, base=0,
                                    pattern=[[-1, P]], channel_multiplier=1).then_inc(ident_ready, 1)
            nc.gpsimd.memset(own_tile[:], 1.0).then_inc(own_tile_ready, 1)
            pool.wait_ge(own_tile_ready, 1)
            nc.gpsimd.affine_select(out=own_tile[:], in_=own_tile[:], compare_op=ALU.is_ge, fill=0.0, base=0,
                                    pattern=[[-2, 2 * NT], [0, P]], channel_multiplier=1).then_inc(own_tile_ready, 1)
            pool.wait_ge(own_tile_ready, 2)
            nc.gpsimd.affine_select(out=own_tile[:], in_=own_tile[:], compare_op=ALU.is_ge, fill=0.0, base=1,
                                    pattern=[[2, 2 * NT], [0, P]], channel_multiplier=-1).then_inc(own_tile_ready, 1)

            def x_low(i, par, h):
                cols = slice(h * HALF, (h + 1) * HALF)
                pool.wait_ge(x_hi_ready[h], upto(1, i, par, 1))
                nc.gpsimd.tensor_tensor(x_lo[:, par, :, cols], x_raw[:, par, :, cols],
                                        x_hi[:, par, :, cols].bitcast(F32), ALU.subtract).then_inc(x_lo_ready, 1)

            for h in range(2):
                x_low(0, 1, h)

            def image(i, par):
                if has_next_but_one(i, par):
                    for h in range(2):
                        x_low(i + 1, par, h)

            over_images(pool, image)

        @block.scalar
        def _(act):
            nc.scalar.preload_act_table_set("natural_log_exp_and_others")
            nc.scalar.preload_act_table_set("natural_log_exp_and_others")
            act.dma_start(taps_sb[:], taps).then_inc(taps_loaded, 16)

            def x_high(i, par, h):
                cols = slice(h * HALF, (h + 1) * HALF)
                act.wait_ge(x_loaded[par], 16 * (i + par))
                if not is_number(i) or i > 0:
                    act.wait_ge(x_used, upto(2, i, par, h - 3))
                nc.scalar.copy(x_hi[:, par, :, cols], x_raw[:, par, :, cols]).then_inc(x_hi_ready[h], 1)

            def theta_high(i, par, h):
                act.wait_ge(thetaphi_done, upto(2, i, par, h + 1))
                nc.scalar.copy(theta_aug[0:2 * K, par, h * HALF:(h + 1) * HALF],
                               thetaphi_ps[h][0:2 * K, :]).then_inc(theta_hi_ready, 1)

            def exp_sums(i, par, h):
                act.wait_ge(neg_max_ready, upto(2, i, par, h + 1))
                tiles = scores_ps[h][:, :, :].rearrange("p a (b m) -> p (a b) m", m=M)
                for t in range(NT):
                    col = h * NT + t
                    last = nc.scalar.activation(tiles[:, t, :], tiles[:, t, :], ACT.Exp,
                                                bias=neg_max[:, col:col + 1], accum_out=exp_sum[:, col:col + 1])
                last.then_inc(exp_sum_ready, 1)

            def ln_sums(i, par):
                act.wait_ge(exp_sum_ready, upto(2, i, par, 2))
                nc.scalar.activation(ln_sum[:], exp_sum[:], ACT.Ln).then_inc(ln_sum_ready, 1)

            def probabilities(i, par, h):
                act.wait_ge(scoresT_done, upto(2, i, par, h + 1))
                nc.scalar.activation(prob[:, h], scores_ps[h][:, :, :], ACT.Exp).then_inc(prob_ready, 1)

            def probabilities_high(i, par, h):
                nc.scalar.activation(prob_hi[:, h], scores_ps[h][:, :, :], ACT.Exp).then_inc(prob_hi_ready, 1)

            def att_high(i, par, h):
                act.wait_ge(att_done, upto(2, i, par, h + 1))
                nc.scalar.copy(att_hi[:, h, :], att_ps[h]).then_inc(att_hi_ready, 1)

            def out_of_psum(i, par, h, f):
                act.wait_ge(out_done, upto(4, i, par, 2 * h + f + 1))
                nc.scalar.copy(y[:, par, f, h * HALF:(h + 1) * HALF], out_ps[h][f]).then_inc(out_evacuated, 1)

            for h in range(2):
                act.wait_ge(x0_loaded[h], 16)
                cols = slice(h * HALF, (h + 1) * HALF)
                nc.scalar.copy(x_hi[:, 0, :, cols], x_raw[:, 0, :, cols]).then_inc(x_hi_ready[h], 1)
            for h in range(2):
                theta_high(0, 0, h)
            for h in range(2):
                x_high(0, 1, h)
            for h in range(2):
                exp_sums(0, 0, h)
            ln_sums(0, 0)

            def image(i, par):
                ni, npar = following(i, par)
                ahead = has_next(i, par)
                probabilities(i, par, 0)
                if ahead:
                    theta_high(ni, npar, 0)
                probabilities_high(i, par, 0)
                probabilities(i, par, 1)
                if ahead:
                    theta_high(ni, npar, 1)
                probabilities_high(i, par, 1)
                att_high(i, par, 0)
                if ahead:
                    exp_sums(ni, npar, 0)
                att_high(i, par, 1)
                if ahead:
                    exp_sums(ni, npar, 1)
                    ln_sums(ni, npar)
                if not (is_number(i) and i == 0):
                    act.wait_ge(y_stored[par], 16 * i)
                for f in range(CT):
                    out_of_psum(i, par, 0, f)
                if has_next_but_one(i, par):
                    x_high(i + 1, par, 1)
                for f in range(CT):
                    out_of_psum(i, par, 1, f)

            over_images(act, image)

        @block.vector
        def _(dve):
            nc.vector.memset(ring_sb[:], 0.0).then_inc(ring_zeroed, 1)
            nc.vector.memset(phi_aug[R_SHIFT:P, :, :].bitcast(F32), 1.0).then_inc(phi_ones_ready, 1)
            dve.wait_ge(taps_loaded, 16)
            dve.wait_ge(ring_zeroed, 1)
            mid = C - 1 - REACH
            nc.vector.tensor_copy(ring_sb[0:1, 0:REACH], taps_sb[0:1, TAPS - REACH:]).then_inc(ring_filled, 1)
            nc.vector.tensor_copy(ring_sb[0:1, mid + C:2 * C - 1], taps_sb[0:1, 0:REACH]).then_inc(ring_filled, 1)
            nc.vector.tensor_copy(ring_sb[0:1, mid:mid + TAPS], taps_sb[0:1, :]).then_inc(ring_filled, 1)
            dve.wait_ge(ring_filled, 3)
            nc.vector.tensor_scalar_add(ring_sb[0:1, C - 1:C], ring_sb[0:1, C - 1:C], 1.0).then_inc(ring_ready, 1)

            dve.wait_ge(proj_w_loaded, 2 * 16)
            twice = tp_raw[:, :, :, :].rearrange("p t a (r k) -> p (t a) r k", r=1).broadcast_to([P, 2 * CT, 2, K])
            tp_hi, tp_lo = (w[:, 0].rearrange("p t (a r k) -> p (t a) r k", a=2, r=2) for w in (w_hi, w_lo))
            nc.vector.tensor_copy(tp_hi, twice).then_inc(proj_w_hi_ready, 1)
            dve.wait_ge(proj_w_hi_ready, 1)
            nc.vector.tensor_tensor(tp_lo, twice, tp_hi.bitcast(F32), ALU.subtract).then_inc(proj_w_ready, 1)
            def band_parts():
                dve.wait_ge(band_loaded, CT * 16)
                nc.vector.tensor_copy(band[:], band_rev[:, :, ::-1]).then_inc(band_ready, 1)
                dve.wait_ge(band_ready, 1)
                nc.vector.tensor_copy(band_hi[:], band[:]).then_inc(band_parts_ready, 1)
                dve.wait_ge(band_parts_ready, 1)
                nc.vector.tensor_tensor(band_lo[:], band[:], band_hi[:].bitcast(F32),
                                        ALU.subtract).then_inc(band_parts_ready, 1)

            def w2_parts():
                dve.wait_ge(w2_done, 1)
                dve.wait_ge(o_loaded, 2 * 16)
                nc.vector.tensor_scalar(w2[:], w2_ps, gamma_sb[:, 0:1], None, ALU.mult).then_inc(w2_scaled, 1)
                dve.wait_ge(w2_scaled, 1)
                nc.vector.tensor_copy(w2_hi[:], w2[:]).then_inc(w2_parts_ready, 1)
                dve.wait_ge(w2_parts_ready, 1)
                nc.vector.tensor_tensor(w2_lo[:], w2[:], w2_hi[:].bitcast(F32), ALU.subtract).then_inc(w2_parts_ready, 1)

            def x_high(i, par, h):
                cols = slice(h * HALF, (h + 1) * HALF)
                dve.wait_ge(x_loaded[par], 16 * (i + par))
                if not is_number(i) or i > 0:
                    dve.wait_ge(x_used, upto(2, i, par, h - 3))
                nc.vector.tensor_copy(x_hi[:, par, :, cols], x_raw[:, par, :, cols]).then_inc(x_hi_ready[h], 1)

            def pool2(dst, src):
                nonlocal_view = src.rearrange("p (r a c b) -> p r c a b", a=2, b=2, c=SIDE // 2)
                return nc.vector.tensor_reduce(dst.rearrange("p (r c) -> p r c", c=SIDE // 2), nonlocal_view,
                                               AXIS.XY, ALU.max)

            def theta_low(i, par, h):
                cols = slice(h * HALF, (h + 1) * HALF)
                dve.wait_ge(theta_hi_ready, upto(2, i, par, h + 1))
                nc.vector.tensor_tensor(theta_aug[2 * K:3 * K, par, cols], thetaphi_ps[h][0:K, :],
                                        theta_aug[0:K, par, cols].bitcast(F32), ALU.subtract).then_inc(theta_lo_ready, 1)

            def pool_phi(i, par, h):
                dve.wait_ge(thetaphi_done, upto(2, i, par, h + 1))
                pool2(phi_pool[:, h * MH:(h + 1) * MH], thetaphi_ps[h][2 * K:4 * K, :]).then_inc(phi_pooled, 1)

            def split_phi(i, par):
                dve.wait_ge(phi_pooled, upto(2, i, par, 2))
                nc.vector.tensor_copy(phi_aug[2 * K:3 * K, par, :], phi_pool[0:K, :])
                nc.vector.tensor_copy(phi_aug[0:2 * K, par, :], phi_pool[:, :]).then_inc(phi_hi_ready, 1)
                dve.wait_ge(phi_hi_ready, upto(1, i, par, 1))
                nc.vector.tensor_tensor(phi_aug[K:2 * K, par, :], phi_pool[K:2 * K, :],
                                        phi_aug[K:2 * K, par, :].bitcast(F32), ALU.subtract).then_inc(phi_ready, 1)

            def pool_g(i, par, h):
                dve.wait_ge(g_done, upto(2, i, par, h + 1))
                pool2(g_pool[:, h * MH:(h + 1) * MH], g_ps[h]).then_inc(g_pooled, 1)

            def split_gT(i, par):
                dve.wait_ge(gT_done, upto(1, i, par, 1))
                nc.vector.tensor_copy(gT_hi[:, :, :], gT_ps.rearrange("p (t c) -> p t c", t=MT)).then_inc(gT_hi_ready, 1)
                dve.wait_ge(gT_hi_ready, upto(1, i, par, 1))
                nc.vector.tensor_tensor(gT_lo[:, :, :], gT_ps.rearrange("p (t c) -> p t c", t=MT),
                                        gT_hi[:, :, :].bitcast(F32), ALU.subtract).then_inc(gT_lo_ready, 1)

            def maxima(i, par, h):
                dve.wait_ge(scores_done, upto(2, i, par, h + 1))
                tiles = scores_ps[h][:, :, :].rearrange("p a (b m) -> p (a b) m", m=M)
                nc.vector.tensor_reduce(neg_max[:, h * NT:(h + 1) * NT], tiles, AXIS.X, ALU.max,
                                        negate=True).then_inc(neg_max_ready, 1)

            def shifts(i, par):
                dve.wait_ge(ln_sum_ready, upto(1, i, par, 1))
                nc.vector.tensor_tensor(shift[:], neg_max[:], ln_sum[:], ALU.subtract).then_inc(shift_ready, 1)
                dve.wait_ge(shift_ready, upto(1, i, par, 1))
                nc.vector.tensor_copy(shift_parts[:, :, 0], shift[:]).then_inc(shift_hi_ready, 1)
                dve.wait_ge(shift_hi_ready, upto(1, i, par, 1))
                nc.vector.tensor_tensor(shift_parts[:, :, 1], shift[:], shift_parts[:, :, 0].bitcast(F32),
                                        ALU.subtract).then_inc(shift_parts_ready, 1)

            def shift_rows(i, par):
                dve.wait_ge(shift_rows_done, upto(1, i, par, 1))
                row = shift_ps[:, :].rearrange("q (o n) -> q o n", o=1).broadcast_to([SHIFT_ROWS, NT, P])
                rows = theta_aug[R_SHIFT:K_AUG, par, :].rearrange("q (t n) -> q t n", n=P)
                for h in range(2):
                    tiles = slice(h * NT, (h + 1) * NT)
                    nc.vector.tensor_tensor(rows[:, tiles, :], row, own_tile[:, tiles, :],
                                            ALU.mult).then_inc(shift_rows_ready, 1)

            def prob_low(i, par, h):
                dve.wait_ge(prob_ready, upto(2, i, par, h + 1))
                dve.wait_ge(prob_hi_ready, upto(2, i, par, h + 1))
                nc.vector.tensor_tensor(prob_lo[:, h], prob[:, h], prob_hi[:, h].bitcast(F32),
                                        ALU.subtract).then_inc(prob_lo_ready, 1)

            def att_low(i, par, h):
                dve.wait_ge(att_hi_ready, upto(2, i, par, h + 1))
                nc.vector.tensor_tensor(att_lo[:, h, :], att_ps[h], att_hi[:, h, :].bitcast(F32),
                                        ALU.subtract).then_inc(att_lo_ready, 1)

            for h in range(2):
                cols = slice(h * HALF, (h + 1) * HALF)
                dve.wait_ge(x_hi_ready[h], 1)
                nc.vector.tensor_tensor(x_lo[:, 0, :, cols], x_raw[:, 0, :, cols], x_hi[:, 0, :, cols].bitcast(F32),
                                        ALU.subtract).then_inc(x_lo_ready, 1)
            dve.wait_ge(g_w_loaded, 16)
            nc.vector.tensor_copy(w_hi[:, 1], g_raw[:]).then_inc(g_w_hi_ready, 1)
            dve.wait_ge(g_w_hi_ready, 1)
            nc.vector.tensor_tensor(w_lo[:, 1], g_raw[:], w_hi[:, 1].bitcast(F32), ALU.subtract).then_inc(g_w_ready, 1)
            for h in range(2):
                pool_phi(0, 0, h)
                theta_low(0, 0, h)
            split_phi(0, 0)
            dve.wait_ge(ident_ready, 1)
            nc.vector.tensor_copy(ident_r[:], ident[:]).then_inc(ident_r_ready, 1)
            maxima(0, 0, 0)
            maxima(0, 0, 1)
            band_parts()
            for h in range(2):
                pool_g(0, 0, h)
            split_gT(0, 0)
            w2_parts()
            shifts(0, 0)
            dve.wait_ge(own_tile_ready, 3)
            shift_rows(0, 0)

            def image(i, par):
                ni, npar = following(i, par)
                ahead = has_next(i, par)
                if ahead:
                    pool_phi(ni, npar, 0)
                    theta_low(ni, npar, 0)
                prob_low(i, par, 0)
                if ahead:
                    pool_phi(ni, npar, 1)
                    theta_low(ni, npar, 1)
                    split_phi(ni, npar)
                prob_low(i, par, 1)
                if ahead:
                    pool_g(ni, npar, 0)
                    maxima(ni, npar, 0)
                att_low(i, par, 0)
                if ahead:
                    maxima(ni, npar, 1)
                    pool_g(ni, npar, 1)
                att_low(i, par, 1)
                if has_next_but_one(i, par):
                    x_high(i + 1, par, 0)
                if ahead:
                    split_gT(ni, npar)
                    shifts(ni, npar)
                    shift_rows(ni, npar)

            over_images(dve, image)

        @block.tensor
        def _(pe):
            def three(dst, w_parts, v_parts, first, last):
                (wh, wl), (vh, vl) = w_parts, v_parts
                nc.tensor.matmul(dst, wh, vh, start=first, stop=False)
                nc.tensor.matmul(dst, wh, vl, start=False, stop=False)
                return nc.tensor.matmul(dst, wl, vh, start=False, stop=last)

            def x_parts(par, t, h):
                cols = slice(h * HALF, (h + 1) * HALF)
                return x_hi[:, par, t, cols], x_lo[:, par, t, cols]

            def project(kind, dst, i, par, h, done):
                pe.wait_ge(x_lo_ready, upto(2, i, par, h + 1))
                for t in range(CT):
                    last = three(dst, (w_hi[:, kind, t, :], w_lo[:, kind, t, :]), x_parts(par, t, h),
                                 t == 0, t == CT - 1)
                last.then_inc(done, 1)

            def theta_phi(i, par, h):
                if not is_number(i) or i > 0:
                    pe.wait_ge(out_evacuated, upto(4, i, par, h - 5))
                elif par == 1:
                    pe.wait_ge(*((theta_lo_ready, 1) if h == 0 else (gT_lo_ready, 1)))
                project(0, thetaphi_ps[h], i, par, h, thetaphi_done)

            def g_projection(i, par, h):
                if h == 0 and (not is_number(i) or i > 0):
                    pe.wait_ge(out_evacuated, upto(4, i, par, -7))
                if h == 1:
                    pe.wait_ge(theta_lo_ready, upto(2, i, par, 2))
                    pe.wait_ge(phi_pooled, upto(2, i, par, 2))
                project(1, g_ps[h], i, par, h, g_done)

            def transpose_g(i, par):
                pe.wait_ge(g_pooled, upto(2, i, par, 2))
                for t in range(MT):
                    last = nc.tensor.transpose(gT_ps[:, t * CG:(t + 1) * CG], g_pool[:, t * P:(t + 1) * P], ident[:])
                last.then_inc(gT_done, 1)

            def scores(i, par, h):
                pe.wait_ge(theta_lo_ready, upto(2, i, par, h + 1))
                pe.wait_ge(phi_ready, upto(1, i, par, 1))
                if not is_first(i, par):
                    pe.wait_ge(prob_hi_ready, upto(2, i, par, h - 1))
                tiles = scores_ps[h][:, :, :].rearrange("p a (b m) -> p (a b) m", m=M)
                for t in range(NT):
                    n0 = h * HALF + t * P
                    last = nc.tensor.matmul(tiles[:, t, :], theta_aug[0:R_SHIFT, par, n0:n0 + P],
                                            phi_aug[0:R_SHIFT, par, :], start=True, stop=True)
                last.then_inc(scores_done, 1)

            def shifts_to_rows(i, par):
                pe.wait_ge(shift_parts_ready, upto(1, i, par, 1))
                nc.tensor.matmul(shift_ps, shift_parts[:, :, :].rearrange("p t s -> p (t s)"), ident_r[:],
                                 start=True, stop=True).then_inc(shift_rows_done, 1)

            def scores_transposed(i, par, h):
                pe.wait_ge(shift_rows_ready, upto(2, i, par, h + 1))
                for t in range(MT):
                    last = nc.tensor.matmul(scores_ps[h][:, t, :], phi_aug[0:K_AUG, par, t * P:(t + 1) * P],
                                            theta_aug[0:K_AUG, par, h * HALF:(h + 1) * HALF], start=True, stop=True)
                last.then_inc(scoresT_done, 1)

            def attend(i, par, h):
                if h == 0:
                    pe.wait_ge(gT_lo_ready, upto(1, i, par, 1))
                    if not is_first(i, par):
                        pe.wait_ge(out_evacuated, upto(4, i, par, -2))
                    else:
                        pe.wait_ge(w2_scaled, 1)
                else:
                    if has_next(i, par):
                        ni, npar = following(i, par)
                        pe.wait_ge(theta_lo_ready, upto(2, ni, npar, 1))
                        pe.wait_ge(phi_pooled, upto(2, ni, npar, 1))
                    else:
                        pe.wait_ge(out_evacuated, upto(4, i, par, -1))
                pe.wait_ge(prob_lo_ready, upto(2, i, par, h + 1))
                for t in range(MT):
                    last = three(att_ps[h], (gT_hi[:, t, :], gT_lo[:, t, :]), (prob_hi[:, h, t, :], prob_lo[:, h, t, :]),
                                 t == 0, t == MT - 1)
                last.then_inc(att_done, 1)

            def filter_x(i, par, h, f):
                if is_first(i, par) and h == 0 and f == 0:
                    pe.wait_ge(band_parts_ready, 2)
                    pe.wait_ge(edge_w_loaded, 6 * 16)
                cols = slice(f * P, (f + 1) * P)
                three(out_ps[h][f], (band_hi[:, f, cols], band_lo[:, f, cols]), x_parts(par, f, h), True, False)
                if h == 0 and f == 0:
                    pe.wait_ge(x_edge_loaded[par], 6 * 16 * (i + 1))
                other = 1 - f
                last = nc.tensor.matmul(out_ps[h][f], edge_w[:, other * P:(other + 1) * P],
                                        x_edge[:, par, other, h * HALF:(h + 1) * HALF], start=False, stop=False)
                if f == CT - 1:
                    last.then_inc(x_used, 1)

            def add_attention(i, par, h, f):
                if is_first(i, par) and h == 0 and f == 0:
                    pe.wait_ge(w2_parts_ready, 2)
                pe.wait_ge(att_lo_ready, upto(2, i, par, h + 1))
                cols = slice(f * P, (f + 1) * P)
                three(out_ps[h][f], (w2_hi[:, cols], w2_lo[:, cols]), (att_hi[:, h, :], att_lo[:, h, :]),
                      False, True).then_inc(out_done, 1)

            pe.wait_ge(proj_w_ready, 1)
            for h in range(2):
                theta_phi(0, 0, h)
            pe.wait_ge(g_w_ready, 1)
            g_projection(0, 0, 0)
            pe.wait_ge(phi_ones_ready, 1)
            for h in range(2):
                scores(0, 0, h)
            g_projection(0, 0, 1)
            theta_phi(0, 1, 0)
            pe.wait_ge(ident_ready, 1)
            transpose_g(0, 0)
            pe.wait_ge(o_loaded, 2 * 16)
            pe.wait_ge(band_ready, 1)
            for t in range(CT):
                last = nc.tensor.matmul(w2_ps, o_sb[:, t, :], band[:, t, :], start=t == 0, stop=t == CT - 1)
            last.then_inc(w2_done, 1)
            pe.wait_ge(g_pooled, 1)
            g_projection(0, 1, 0)
            pe.wait_ge(ident_r_ready, 1)
            shifts_to_rows(0, 0)

            def image(i, par):
                ni, npar = following(i, par)
                ahead = has_next(i, par)
                scores_transposed(i, par, 0)
                if ahead and not is_first(i, par):
                    theta_phi(ni, npar, 0)
                scores_transposed(i, par, 1)
                if ahead:
                    theta_phi(ni, npar, 1)
                if ahead and not is_first(i, par):
                    g_projection(ni, npar, 0)
                attend(i, par, 0)
                if ahead:
                    g_projection(ni, npar, 1)
                    scores(ni, npar, 0)
                attend(i, par, 1)
                if ahead:
                    scores(ni, npar, 1)
                if ahead:
                    pe.wait_ge(g_pooled, upto(2, ni, npar, 1))
                filter_x(i, par, 0, 0)
                pe.wait_ge(att_lo_ready, upto(2, i, par, 1))
                filter_x(i, par, 0, 1)
                for f in range(CT):
                    add_attention(i, par, 0, f)
                if ahead:
                    transpose_g(ni, npar)
                pe.wait_ge(att_lo_ready, upto(2, i, par, 2))
                filter_x(i, par, 1, 0)
                if ahead:
                    pe.wait_ge(gT_lo_ready, upto(1, ni, npar, 1))
                filter_x(i, par, 1, 1)
                if ahead:
                    shifts_to_rows(ni, npar)
                for f in range(CT):
                    add_attention(i, par, 1, f)

            over_images(pe, image)


def kernel(x, L0_conv_theta_w, L0_conv_phi_w, L0_conv_g_w, L0_conv_o_w, L0_conv_gamma, L1_conv_inhibition_filter):
    import numpy as np
    import concourse.bacc as bacc
    from concourse.bass_utils import run_bass_kernel_spmd

    x = np.asarray(x)
    B, C, H, W = x.shape
    arrays = {
        "x": np.ascontiguousarray(x).reshape(B, C, H * W),
        "theta_wT": np.ascontiguousarray(np.asarray(L0_conv_theta_w).T),
        "phi_wT": np.ascontiguousarray(np.asarray(L0_conv_phi_w).T),
        "g_wT": np.ascontiguousarray(np.asarray(L0_conv_g_w).T),
        "o_w": np.ascontiguousarray(np.asarray(L0_conv_o_w)),
        "gamma": np.asarray(L0_conv_gamma).reshape(1),
        "taps": np.asarray(L1_conv_inhibition_filter).reshape(1, -1),
    }
    nc = bacc.Bacc("TRN2", target_bir_lowering=False, num_devices=1)
    aps = [nc.dram_tensor(name, a.shape, mybir.dt.from_np(a.dtype), kind="ExternalInput").ap()
           for name, a in arrays.items()]
    out = nc.dram_tensor("out", (B, C, H * W), F32, kind="ExternalOutput").ap()
    ring = nc.dram_tensor("ring", (1, 2 * C), F32, kind="Internal").ap()
    attention_then_channel_filter(nc, *aps, out, ring)
    got = run_bass_kernel_spmd(nc, [arrays], core_ids=[0])
    return got.results[0]["out"].reshape(B, C, H, W)
```

```python
from contextlib import ExitStack

import concourse.bass as bass
from concourse import mybir

ALU = mybir.AluOpType
ACT = mybir.ActivationFunctionType
AXIS = mybir.AxisListType
F32 = mybir.dt.float32
F32R = mybir.dt.float32r

P = 128


def attention_then_channel_filter(nc, x, theta_wT, phi_wT, g_wT, o_w, gamma, taps, out, ring):
    B, C, HW = x.shape
    K = theta_wT.shape[1]
    CG = g_wT.shape[1]
    SIDE = 32
    M = HW // 4
    TAPS = taps.shape[1]
    CT = C // P
    MT = M // P
    HALF = HW // 2
    NT = HALF // P
    MH = M // 2
    R_SHIFT = 3 * K
    SHIFT_ROWS = 2 * 2 * NT
    K_AUG = R_SHIFT + SHIFT_ROWS
    REACH = TAPS // 2
    K_EDGE = 3 * 2 * REACH
    EDGE_LOADS = 3 * 2 * 16
    assert HW == SIDE * SIDE and C == 2 * P and CG == P and K == 32 and HALF == 512
    PAIRS = B // 2

    x_v = x.rearrange("b (t p) n -> b p t n", p=P)
    out_v = out.rearrange("b (t p) n -> b p t n", p=P)

    with ExitStack() as ctx:
        def sb(name, shape, dt=F32):
            return ctx.enter_context(nc.sbuf_tensor(name, shape, dt))

        def sem(name):
            return ctx.enter_context(nc.semaphore(name))

        tp_raw = sb("tp_raw", [P, CT, 2, K])
        g_raw = sb("g_raw", [P, CT, P])
        tp_w = sb("tp_w", [P, CT, 4, K], F32R)
        g_hi_w = sb("g_hi_w", [P, CT, CG], F32R)
        g_lo_w = sb("g_lo_w", [P, CT, CG], F32R)
        o_sb = sb("o_sb", [P, CT, CG])
        gamma_sb = sb("gamma_sb", [P, 1])
        taps_sb = sb("taps_sb", [1, TAPS])
        ring_sb = sb("ring_sb", [1, 2 * C])
        band_rev = sb("band_rev", [P, CT, C])
        band = sb("band", [P, CT, C])
        band_hi = sb("band_hi", [P, CT, C], F32R)
        band_lo = sb("band_lo", [P, CT, C], F32R)
        edge_w = sb("edge_w", [K_EDGE, CT * P], F32R)
        w2 = sb("w2", [P, C])
        w2_hi = sb("w2_hi", [P, C], F32R)
        w2_lo = sb("w2_lo", [P, C], F32R)
        ident = sb("ident", [P, P])
        ident_r = sb("ident_r", [P, P], F32R)
        own_tile = sb("own_tile", [SHIFT_ROWS, 2 * NT, P])

        x_raw = sb("x_raw", [P, 2, CT, HW])
        x_hi = sb("x_hi", [P, 2, CT, HW], F32R)
        x_lo = sb("x_lo", [P, 2, CT, HW], F32R)
        x_edge = sb("x_edge", [K_EDGE, 2, CT, HW], F32R)
        theta_aug = sb("theta_aug", [P, 2, HW], F32R)
        phi_aug = sb("phi_aug", [P, 2, M], F32R)
        thetaphi = sb("thetaphi", [2 * K, 2, HALF])
        thetaphi_rest = sb("thetaphi_rest", [2 * K, 2, HALF])
        phi_pool = sb("phi_pool", [K, M])
        g_pool = sb("g_pool", [P, M])
        g_hi = sb("g_hi", [P, M], F32R)
        g_lo = sb("g_lo", [P, M], F32R)
        value_hi = sb("value_hi", [P, 2, MT, C], F32R)
        value_lo = sb("value_lo", [P, 2, MT, C], F32R)
        neg_max = sb("neg_max", [P, 2 * NT])
        exp_sum = sb("exp_sum", [P, 2 * NT])
        ln_sum = sb("ln_sum", [P, 2 * NT])
        shift = sb("shift", [P, 2 * NT])
        shift_parts = sb("shift_parts", [P, 2 * NT, 2], F32R)
        prob = sb("prob", [P, 2, MT, HALF])
        prob_hi = sb("prob_hi", [P, 2, MT, HALF], F32R)
        prob_lo = sb("prob_lo", [P, 2, MT, HALF], F32R)
        y = sb("y", [P, 2, CT, HW])

        psX = ctx.enter_context(nc.psum_tensor("psX", [P, 2, HALF], F32))
        psZ = ctx.enter_context(nc.psum_tensor("psZ", [P, 2, HALF], F32))
        psY = ctx.enter_context(nc.psum_tensor("psY", [P, 2, HALF], F32))
        psV = ctx.enter_context(nc.psum_tensor("psV", [P, 2, HALF], F32))
        scores_ps = [psX, psZ]
        thetaphi_ps = [psY[:, 0, :], psY[:, 1, :]]
        g_ps = [psV[:, 0, :], psY[:, 0, :]]
        value_ps = psV[:, 1, :]
        out_ps = [[psV[:, 1, :], psV[:, 0, :]], [psY[:, 1, :], psV[:, 0, :]]]
        last_out_ps = [out_ps[0], [psY[:, 1, :], psY[:, 0, :]]]
        w2_ps = psV[:, 1, 0:C]
        shift_ps = psZ[0:SHIFT_ROWS, 0, 0:P]

        proj_w_loaded = sem("proj_w_loaded")
        g_w_loaded = sem("g_w_loaded")
        g_w_hi_ready = sem("g_w_hi_ready")
        g_w_ready = sem("g_w_ready")
        o_loaded = sem("o_loaded")
        taps_loaded = sem("taps_loaded")
        ring_zeroed = sem("ring_zeroed")
        ring_filled = sem("ring_filled")
        ring_ready = sem("ring_ready")
        ring_stored = sem("ring_stored")
        band_loaded = sem("band_loaded")
        band_ready = sem("band_ready")
        proj_w_hi_ready = sem("proj_w_hi_ready")
        proj_w_ready = sem("proj_w_ready")
        band_parts_ready = sem("band_parts_ready")
        edge_w_loaded = sem("edge_w_loaded")
        w2_done = sem("w2_done")
        w2_scaled = sem("w2_scaled")
        w2_hi_ready = sem("w2_hi_ready")
        w2_ready = sem("w2_ready")
        ident_zeroed = sem("ident_zeroed")
        ident_ready = sem("ident_ready")
        ident_r_ready = sem("ident_r_ready")
        own_tile_ready = sem("own_tile_ready")
        phi_ones_ready = sem("phi_ones_ready")

        x0_loaded = [sem("x0_loaded0"), sem("x0_loaded1")]
        x_loaded = [sem("x_loaded0"), sem("x_loaded1")]
        x_hi_ready = [sem("x_hi_ready0"), sem("x_hi_ready1")]
        x_lo_ready = [sem("x_lo_ready0"), sem("x_lo_ready1")]
        x_edge_loaded = [sem("x_edge_loaded0"), sem("x_edge_loaded1")]
        thetaphi_done = sem("thetaphi_done")
        thetaphi_rest_ready = sem("thetaphi_rest_ready")
        thetaphi_summed = sem("thetaphi_summed")
        theta_hi_ready = sem("theta_hi_ready")
        theta_lo_ready = sem("theta_lo_ready")
        phi_pooled = sem("phi_pooled")
        phi_hi_ready = sem("phi_hi_ready")
        phi_ready = sem("phi_ready")
        g_done = sem("g_done")
        g_pooled = sem("g_pooled")
        g_hi_ready = sem("g_hi_ready")
        g_lo_ready = sem("g_lo_ready")
        value_done = sem("value_done")
        value_hi_ready = sem("value_hi_ready")
        value_lo_ready = sem("value_lo_ready")
        scores_done = sem("scores_done")
        neg_max_ready = sem("neg_max_ready")
        exp_sum_ready = sem("exp_sum_ready")
        ln_sum_ready = sem("ln_sum_ready")
        shift_ready = sem("shift_ready")
        shift_hi_ready = sem("shift_hi_ready")
        shift_parts_ready = sem("shift_parts_ready")
        shift_rows_done = sem("shift_rows_done")
        shift_rows_ready = sem("shift_rows_ready")
        scoresT_done = sem("scoresT_done")
        prob_ready = sem("prob_ready")
        prob_hi_ready = sem("prob_hi_ready")
        prob_lo_ready = sem("prob_lo_ready")
        x_used = sem("x_used")
        out_done = sem("out_done")
        out_evacuated = [[sem(f"out_evacuated{h}{f}") for f in range(CT)] for h in range(2)]
        y_stored = [sem("y_stored0"), sem("y_stored1")]

        block = ctx.enter_context(nc.Block())

        def upto(per_image, i, par, within):
            return i * (2 * per_image) + (par * per_image + within)

        def following(i, par):
            return (i, 1) if par == 0 else (i + 1, 0)

        def over_images(engine, image):
            image(0, 0)
            image(0, 1)
            with engine.Fori(1, PAIRS - 1) as i:
                image(i, 0)
                image(i, 1)
            image(PAIRS - 1, 0)
            image(PAIRS - 1, 1)

        def is_number(i):
            return isinstance(i, int)

        def has_next(i, par):
            return not (is_number(i) and i == PAIRS - 1 and par == 1)

        def has_next_but_one(i, par):
            return not (is_number(i) and i == PAIRS - 1)

        def is_last(i, par):
            return not has_next(i, par)

        def is_first(i, par):
            return is_number(i) and i == 0 and par == 0

        @block.sync
        def _(sp):
            def load(i, par):
                sp.dma_start(x_raw[:, par], x_v[2 * i + par]).then_inc(x_loaded[par], 16)

            sp.dma_start(x_raw[:, 0, :, 0:HALF], x_v[0][:, :, 0:HALF]).then_inc(x0_loaded[0], 16)
            sp.dma_start(tp_raw[:, :, 0, :], theta_wT.rearrange("(t p) k -> p t k", p=P)).then_inc(proj_w_loaded, 16)
            sp.dma_start(tp_raw[:, :, 1, :], phi_wT.rearrange("(t p) k -> p t k", p=P)).then_inc(proj_w_loaded, 16)
            sp.dma_start(x_raw[:, 0, :, HALF:HW], x_v[0][:, :, HALF:HW]).then_inc(x0_loaded[1], 16)
            sp.dma_start(g_raw[:], g_wT.rearrange("(t p) k -> p t k", p=P)).then_inc(g_w_loaded, 16)
            sp.wait_ge(ring_ready, 1)
            sp.dma_start(ring, ring_sb[0:1, :]).then_inc(ring_stored, 16)
            sp.wait_ge(ring_stored, 16)
            for t in range(CT):
                diagonals = bass.AP(tensor=ring.tensor, offset=t * P, ap=[[1, P], [1, C]])
                sp.dma_start(band_rev[:, t, :], diagonals).then_inc(band_loaded, 16)
            load(0, 1)

            def stack_edges(dst, loaded, parts):
                for n, part in enumerate(parts):
                    for e, rows in enumerate((slice(0, REACH), slice(P - REACH, P))):
                        row = (2 * n + e) * REACH
                        sp.dma_start(dst[row:row + REACH].bitcast(F32), part[rows].bitcast(F32)).then_inc(loaded, 16)

            def x_edges(i, par):
                for h in range(2):
                    sp.wait_ge(x_lo_ready[h], upto(1, i, par, 1))
                stack_edges(x_edge[:, par], x_edge_loaded[par], (x_hi[:, par], x_lo[:, par], x_hi[:, par]))

            x_edges(0, 0)
            sp.wait_ge(band_parts_ready, 2)
            hi, lo = (b[:, :, :].rearrange("p t c -> p (t c)")[:, P:P + CT * P] for b in (band_hi, band_lo))
            stack_edges(edge_w[:, :], edge_w_loaded, (hi, hi, lo))

            def image(i, par):
                if has_next(i, par):
                    x_edges(*following(i, par))
                if has_next_but_one(i, par):
                    for h in range(2):
                        sp.wait_ge(x_lo_ready[h], upto(1, i, par, 1))
                    load(i + 1, par)
                if has_next(i, par):
                    sp.wait_ge(out_evacuated[1][1], upto(1, i, par, 1))
                    sp.dma_start(out_v[2 * i + par], y[:, par]).then_inc(y_stored[par], 16)
                else:
                    for h in range(2):
                        for f in range(CT):
                            cols = slice(h * HALF, (h + 1) * HALF)
                            sp.wait_ge(out_evacuated[h][f], upto(1, i, par, 1))
                            sp.dma_start(out_v[2 * i + par][:, f, cols], y[:, par, f, cols]).then_inc(y_stored[par], 16)

            over_images(sp, image)
            sp.wait_ge(y_stored[0], 16 * PAIRS)
            sp.wait_ge(y_stored[1], 16 * (PAIRS - 1 + 4))

        @block.gpsimd
        def _(pool):
            pool.dma_start(o_sb[:], o_w.rearrange("(t p) k -> p t k", p=P)).then_inc(o_loaded, 16)
            pool.dma_start(gamma_sb[:], gamma.partition_broadcast(P)).then_inc(o_loaded, 16)
            nc.gpsimd.memset(ident[:], 0.0).then_inc(ident_zeroed, 1)
            pool.wait_ge(ident_zeroed, 1)
            nc.gpsimd.affine_select(out=ident[:], in_=ident[:], compare_op=ALU.not_equal, fill=1.0, base=0,
                                    pattern=[[-1, P]], channel_multiplier=1).then_inc(ident_ready, 1)
            nc.gpsimd.memset(own_tile[:], 1.0).then_inc(own_tile_ready, 1)
            pool.wait_ge(own_tile_ready, 1)
            nc.gpsimd.affine_select(out=own_tile[:], in_=own_tile[:], compare_op=ALU.is_ge, fill=0.0, base=0,
                                    pattern=[[-2, 2 * NT], [0, P]], channel_multiplier=1).then_inc(own_tile_ready, 1)
            pool.wait_ge(own_tile_ready, 2)
            nc.gpsimd.affine_select(out=own_tile[:], in_=own_tile[:], compare_op=ALU.is_ge, fill=0.0, base=1,
                                    pattern=[[2, 2 * NT], [0, P]], channel_multiplier=-1).then_inc(own_tile_ready, 1)

            pool.wait_ge(band_loaded, CT * 16)
            nc.gpsimd.tensor_copy(band[:], band_rev[:, :, ::-1]).then_inc(band_ready, 1)
            pool.wait_ge(band_ready, 1)
            nc.gpsimd.tensor_copy(band_hi[:], band[:]).then_inc(band_parts_ready, 1)
            pool.wait_ge(band_parts_ready, 1)
            nc.gpsimd.tensor_tensor(band_lo[:], band[:], band_hi[:].bitcast(F32), ALU.subtract).then_inc(band_parts_ready, 1)

            def x_low_of_half_0(i, par):
                cols = slice(0, HALF)
                pool.wait_ge(x_hi_ready[0], upto(1, i, par, 1))
                nc.gpsimd.tensor_tensor(x_lo[:, par, :, cols], x_raw[:, par, :, cols],
                                        x_hi[:, par, :, cols].bitcast(F32), ALU.subtract).then_inc(x_lo_ready[0], 1)

            def prob_low(i, par, h):
                pool.wait_ge(prob_hi_ready, upto(2, i, par, h + 1))
                nc.gpsimd.tensor_tensor(prob_lo[:, h], prob[:, h], prob_hi[:, h].bitcast(F32),
                                        ALU.subtract).then_inc(prob_lo_ready, 1)

            x_low_of_half_0(0, 1)
            pool.wait_ge(w2_scaled, 1)
            pool.wait_ge(w2_hi_ready, 1)
            nc.gpsimd.tensor_tensor(w2_lo[:], w2[:], w2_hi[:].bitcast(F32), ALU.subtract).then_inc(w2_ready, 1)

            def image(i, par):
                if has_next(i, par):
                    for h in range(2):
                        prob_low(i, par, h)
                if has_next_but_one(i, par):
                    x_low_of_half_0(i + 1, par)

            over_images(pool, image)

        @block.scalar
        def _(act):
            nc.scalar.preload_act_table_set("natural_log_exp_and_others")
            act.dma_start(taps_sb[:], taps).then_inc(taps_loaded, 16)

            def x_high(i, par, h):
                cols = slice(h * HALF, (h + 1) * HALF)
                act.wait_ge(x_loaded[par], 16 * (i + par))
                if not is_number(i) or i > 0:
                    act.wait_ge(x_used, upto(2, i, par, h - 3))
                nc.scalar.copy(x_hi[:, par, :, cols], x_raw[:, par, :, cols]).then_inc(x_hi_ready[h], 1)

            def take_thetaphi_rest(i, par, h):
                act.wait_ge(thetaphi_done, upto(2, i, par, h + 1))
                nc.scalar.copy(thetaphi_rest[:, h, :], thetaphi_ps[h][2 * K:4 * K, :]).then_inc(thetaphi_rest_ready, 1)

            def theta_high(i, par, h):
                act.wait_ge(thetaphi_summed, upto(2, i, par, h + 1))
                for rows in (slice(0, K), slice(K, 2 * K)):
                    nc.scalar.copy(theta_aug[rows, par, h * HALF:(h + 1) * HALF],
                                   thetaphi[0:K, h, :]).then_inc(theta_hi_ready, 1)

            def exp_sums(i, par, h):
                act.wait_ge(neg_max_ready, upto(2, i, par, h + 1))
                tiles = scores_ps[h][:, :, :].rearrange("p a (b m) -> p (a b) m", m=M)
                for t in range(NT):
                    col = h * NT + t
                    last = nc.scalar.activation(tiles[:, t, :], tiles[:, t, :], ACT.Exp,
                                                bias=neg_max[:, col:col + 1], accum_out=exp_sum[:, col:col + 1])
                last.then_inc(exp_sum_ready, 1)

            def ln_sums(i, par):
                act.wait_ge(exp_sum_ready, upto(2, i, par, 2))
                nc.scalar.activation(ln_sum[:], exp_sum[:], ACT.Ln).then_inc(ln_sum_ready, 1)

            def probabilities(i, par, h):
                act.wait_ge(scoresT_done, upto(2, i, par, h + 1))
                nc.scalar.activation(prob[:, h], scores_ps[h][:, :, :], ACT.Exp).then_inc(prob_ready, 1)

            def probabilities_high(i, par, h):
                nc.scalar.activation(prob_hi[:, h], scores_ps[h][:, :, :], ACT.Exp).then_inc(prob_hi_ready, 1)

            def value_high(i, par):
                act.wait_ge(value_done, upto(1, i, par, 1))
                nc.scalar.copy(value_hi[:, par], value_ps.rearrange("p (t c) -> p t c", t=MT)).then_inc(value_hi_ready, 1)

            def out_of_psum(i, par, h, f):
                act.wait_ge(out_done, upto(4, i, par, 2 * h + f + 1))
                if (h, f) == (0, 0) and not (is_number(i) and i == 0):
                    act.wait_ge(y_stored[par], 16 * i)
                bank = (last_out_ps if is_last(i, par) else out_ps)[h][f]
                nc.scalar.copy(y[:, par, f, h * HALF:(h + 1) * HALF], bank).then_inc(out_evacuated[h][f], 1)

            act.wait_ge(x0_loaded[1], 16)
            nc.scalar.copy(x_hi[:, 0, :, HALF:HW], x_raw[:, 0, :, HALF:HW]).then_inc(x_hi_ready[1], 1)
            for h in range(2):
                take_thetaphi_rest(0, 0, h)
            for h in range(2):
                theta_high(0, 0, h)
            for h in range(2):
                x_high(0, 1, h)
            act.wait_ge(w2_done, 1)
            act.wait_ge(o_loaded, 2 * 16)
            nc.scalar.activation(w2[:], w2_ps, ACT.Identity, scale=gamma_sb[:, 0:1]).then_inc(w2_scaled, 1)
            nc.scalar.activation(w2_hi[:], w2_ps, ACT.Identity, scale=gamma_sb[:, 0:1]).then_inc(w2_hi_ready, 1)
            for h in range(2):
                exp_sums(0, 0, h)
            ln_sums(0, 0)
            for h in range(2):
                take_thetaphi_rest(0, 1, h)
            value_high(0, 0)
            theta_high(0, 1, 0)

            def image(i, par):
                ni, npar = following(i, par)
                ahead = has_next(i, par)
                probabilities(i, par, 0)
                if ahead and not is_first(i, par):
                    take_thetaphi_rest(ni, npar, 0)
                probabilities_high(i, par, 0)
                if ahead and not is_first(i, par):
                    take_thetaphi_rest(ni, npar, 1)
                    theta_high(ni, npar, 0)
                if ahead:
                    theta_high(ni, npar, 1)
                probabilities(i, par, 1)
                probabilities_high(i, par, 1)
                if ahead:
                    exp_sums(ni, npar, 0)
                out_of_psum(i, par, 0, 0)
                if ahead:
                    exp_sums(ni, npar, 1)
                    ln_sums(ni, npar)
                out_of_psum(i, par, 1, 0)
                if ahead:
                    value_high(ni, npar)
                if has_next_but_one(i, par):
                    x_high(i + 1, par, 1)
                out_of_psum(i, par, 1, 1)

            over_images(act, image)

        @block.vector
        def _(dve):
            nc.vector.memset(ring_sb[:], 0.0).then_inc(ring_zeroed, 1)
            nc.vector.memset(phi_aug[R_SHIFT:P, :, :].bitcast(F32), 1.0).then_inc(phi_ones_ready, 1)
            dve.wait_ge(taps_loaded, 16)
            dve.wait_ge(ring_zeroed, 1)
            mid = C - 1 - REACH
            nc.vector.tensor_copy(ring_sb[0:1, 0:REACH], taps_sb[0:1, TAPS - REACH:]).then_inc(ring_filled, 1)
            nc.vector.tensor_copy(ring_sb[0:1, mid + C:2 * C - 1], taps_sb[0:1, 0:REACH]).then_inc(ring_filled, 1)
            nc.vector.tensor_copy(ring_sb[0:1, mid:mid + TAPS], taps_sb[0:1, :]).then_inc(ring_filled, 1)
            dve.wait_ge(ring_filled, 3)
            nc.vector.tensor_scalar_add(ring_sb[0:1, C - 1:C], ring_sb[0:1, C - 1:C], 1.0).then_inc(ring_ready, 1)

            dve.wait_ge(proj_w_loaded, 2 * 16)
            nc.vector.tensor_copy(tp_w[:, :, 0:2], tp_raw[:]).then_inc(proj_w_hi_ready, 1)
            dve.wait_ge(proj_w_hi_ready, 1)
            nc.vector.tensor_tensor(tp_w[:, :, 2:4], tp_raw[:], tp_w[:, :, 0:2].bitcast(F32),
                                    ALU.subtract).then_inc(proj_w_ready, 1)

            def x_high(i, par, h):
                cols = slice(h * HALF, (h + 1) * HALF)
                dve.wait_ge(x_loaded[par], 16 * (i + par))
                if not is_number(i) or i > 0:
                    dve.wait_ge(x_used, upto(2, i, par, h - 3))
                nc.vector.tensor_copy(x_hi[:, par, :, cols], x_raw[:, par, :, cols]).then_inc(x_hi_ready[h], 1)

            def x_low_of_half_1(i, par):
                cols = slice(HALF, HW)
                dve.wait_ge(x_hi_ready[1], upto(1, i, par, 1))
                nc.vector.tensor_tensor(x_lo[:, par, :, cols], x_raw[:, par, :, cols], x_hi[:, par, :, cols].bitcast(F32),
                                        ALU.subtract).then_inc(x_lo_ready[1], 1)

            def pool2(dst, src):
                return nc.vector.tensor_reduce(dst.rearrange("p (r c) -> p r c", c=SIDE // 2),
                                               src.rearrange("p (r a c b) -> p r c a b", a=2, b=2, c=SIDE // 2),
                                               AXIS.XY, ALU.max)

            def sum_thetaphi(i, par, h):
                dve.wait_ge(thetaphi_rest_ready, upto(2, i, par, h + 1))
                nc.vector.tensor_tensor(thetaphi[:, h, :], thetaphi_ps[h][0:2 * K, :], thetaphi_rest[:, h, :],
                                        ALU.add).then_inc(thetaphi_summed, 1)

            def theta_low(i, par, h):
                cols = slice(h * HALF, (h + 1) * HALF)
                dve.wait_ge(theta_hi_ready, upto(4, i, par, 2 * h + 2))
                nc.vector.tensor_tensor(theta_aug[2 * K:3 * K, par, cols], thetaphi[0:K, h, :],
                                        theta_aug[0:K, par, cols].bitcast(F32), ALU.subtract).then_inc(theta_lo_ready, 1)

            def pool_phi(i, par, h):
                dve.wait_ge(thetaphi_summed, upto(2, i, par, h + 1))
                pool2(phi_pool[:, h * MH:(h + 1) * MH], thetaphi[K:2 * K, h, :]).then_inc(phi_pooled, 1)

            def split_phi(i, par):
                dve.wait_ge(phi_pooled, upto(2, i, par, 2))
                for rows in (slice(0, K), slice(2 * K, 3 * K)):
                    nc.vector.tensor_copy(phi_aug[rows, par, :], phi_pool[:]).then_inc(phi_hi_ready, 1)
                dve.wait_ge(phi_hi_ready, upto(2, i, par, 2))
                nc.vector.tensor_tensor(phi_aug[K:2 * K, par, :], phi_pool[:], phi_aug[0:K, par, :].bitcast(F32),
                                        ALU.subtract).then_inc(phi_ready, 1)

            def pool_g(i, par, h):
                dve.wait_ge(g_done, upto(2, i, par, h + 1))
                pool2(g_pool[:, h * MH:(h + 1) * MH], g_ps[h]).then_inc(g_pooled, 1)

            def split_g(i, par):
                dve.wait_ge(g_pooled, upto(2, i, par, 2))
                nc.vector.tensor_copy(g_hi[:], g_pool[:]).then_inc(g_hi_ready, 1)
                dve.wait_ge(g_hi_ready, upto(1, i, par, 1))
                nc.vector.tensor_tensor(g_lo[:], g_pool[:], g_hi[:].bitcast(F32), ALU.subtract).then_inc(g_lo_ready, 1)

            def value_low(i, par):
                dve.wait_ge(value_hi_ready, upto(1, i, par, 1))
                nc.vector.tensor_tensor(value_lo[:, par], value_ps.rearrange("p (t c) -> p t c", t=MT),
                                        value_hi[:, par].bitcast(F32), ALU.subtract).then_inc(value_lo_ready, 1)

            def out_of_psum(i, par):
                dve.wait_ge(out_done, upto(4, i, par, 2))
                if not (is_number(i) and i == 0):
                    dve.wait_ge(y_stored[par], 16 * i)
                nc.vector.tensor_copy(y[:, par, 1, 0:HALF], out_ps[0][1]).then_inc(out_evacuated[0][1], 1)

            def prob_low(i, par, h):
                dve.wait_ge(prob_hi_ready, upto(2, i, par, h + 1))
                nc.vector.tensor_tensor(prob_lo[:, h], prob[:, h], prob_hi[:, h].bitcast(F32),
                                        ALU.subtract).then_inc(prob_lo_ready, 1)

            def maxima(i, par, h):
                dve.wait_ge(scores_done, upto(2, i, par, h + 1))
                tiles = scores_ps[h][:, :, :].rearrange("p a (b m) -> p (a b) m", m=M)
                nc.vector.tensor_reduce(neg_max[:, h * NT:(h + 1) * NT], tiles, AXIS.X, ALU.max,
                                        negate=True).then_inc(neg_max_ready, 1)

            def shifts(i, par):
                dve.wait_ge(ln_sum_ready, upto(1, i, par, 1))
                nc.vector.tensor_tensor(shift[:], neg_max[:], ln_sum[:], ALU.subtract).then_inc(shift_ready, 1)
                dve.wait_ge(shift_ready, upto(1, i, par, 1))
                nc.vector.tensor_copy(shift_parts[:, :, 0], shift[:]).then_inc(shift_hi_ready, 1)
                dve.wait_ge(shift_hi_ready, upto(1, i, par, 1))
                nc.vector.tensor_tensor(shift_parts[:, :, 1], shift[:], shift_parts[:, :, 0].bitcast(F32),
                                        ALU.subtract).then_inc(shift_parts_ready, 1)

            def shift_rows(i, par, h):
                dve.wait_ge(shift_rows_done, upto(1, i, par, 1))
                row = shift_ps[:, :].rearrange("q (o n) -> q o n", o=1).broadcast_to([SHIFT_ROWS, NT, P])
                rows = theta_aug[R_SHIFT:K_AUG, par, :].rearrange("q (t n) -> q t n", n=P)
                tiles = slice(h * NT, (h + 1) * NT)
                nc.vector.tensor_tensor(rows[:, tiles, :], row, own_tile[:, tiles, :],
                                        ALU.mult).then_inc(shift_rows_ready, 1)

            dve.wait_ge(ident_ready, 1)
            nc.vector.tensor_copy(ident_r[:], ident[:]).then_inc(ident_r_ready, 1)

            dve.wait_ge(x0_loaded[0], 16)
            nc.vector.tensor_copy(x_hi[:, 0, :, 0:HALF], x_raw[:, 0, :, 0:HALF]).then_inc(x_hi_ready[0], 1)
            for h in range(2):
                cols = slice(h * HALF, (h + 1) * HALF)
                dve.wait_ge(x_hi_ready[h], 1)
                nc.vector.tensor_tensor(x_lo[:, 0, :, cols], x_raw[:, 0, :, cols], x_hi[:, 0, :, cols].bitcast(F32),
                                        ALU.subtract).then_inc(x_lo_ready[h], 1)
            dve.wait_ge(g_w_loaded, 16)
            nc.vector.tensor_copy(g_hi_w[:], g_raw[:]).then_inc(g_w_hi_ready, 1)
            dve.wait_ge(g_w_hi_ready, 1)
            nc.vector.tensor_tensor(g_lo_w[:], g_raw[:], g_hi_w[:].bitcast(F32), ALU.subtract).then_inc(g_w_ready, 1)
            for h in range(2):
                sum_thetaphi(0, 0, h)
                pool_phi(0, 0, h)
            theta_low(0, 0, 0)
            split_phi(0, 0)
            theta_low(0, 0, 1)
            maxima(0, 0, 0)
            pool_g(0, 0, 0)
            maxima(0, 0, 1)
            pool_g(0, 0, 1)
            x_low_of_half_1(0, 1)
            split_g(0, 0)
            shifts(0, 0)
            sum_thetaphi(0, 1, 0)
            dve.wait_ge(own_tile_ready, 3)
            for h in range(2):
                shift_rows(0, 0, h)
            value_low(0, 0)

            def image(i, par):
                ni, npar = following(i, par)
                if not has_next(i, par):
                    for h in range(2):
                        prob_low(i, par, h)
                    out_of_psum(i, par)
                    return
                if not is_first(i, par):
                    sum_thetaphi(ni, npar, 0)
                pool_phi(ni, npar, 0)
                sum_thetaphi(ni, npar, 1)
                pool_phi(ni, npar, 1)
                theta_low(ni, npar, 0)
                split_phi(ni, npar)
                theta_low(ni, npar, 1)
                pool_g(ni, npar, 0)
                for h in range(2):
                    maxima(ni, npar, h)
                pool_g(ni, npar, 1)
                split_g(ni, npar)
                if has_next_but_one(i, par):
                    x_high(i + 1, par, 0)
                out_of_psum(i, par)
                shifts(ni, npar)
                for h in range(2):
                    shift_rows(ni, npar, h)
                if has_next_but_one(i, par):
                    x_low_of_half_1(i + 1, par)
                value_low(ni, npar)

            over_images(dve, image)

        @block.tensor
        def _(pe):
            def three(dst, w_parts, v_parts, first, last):
                (wh, wl), (vh, vl) = w_parts, v_parts
                nc.tensor.matmul(dst, wh, vh, start=first, stop=False)
                nc.tensor.matmul(dst, wh, vl, start=False, stop=False)
                return nc.tensor.matmul(dst, wl, vh, start=False, stop=last)

            def x_parts(par, t, h):
                cols = slice(h * HALF, (h + 1) * HALF)
                return x_hi[:, par, t, cols], x_lo[:, par, t, cols]

            def theta_phi(i, par, h):
                if h == 0 and not is_first(i, par):
                    pe.wait_ge(g_pooled, upto(2, i, par, 0))
                elif h == 1 and (not is_number(i) or i > 0):
                    pe.wait_ge(out_evacuated[1][0], upto(1, i, par, -1))
                elif h == 1 and par == 1:
                    pe.wait_ge(thetaphi_summed, 2)
                cols = slice(h * HALF, (h + 1) * HALF)
                for part, ready in ((x_hi, x_hi_ready), (x_lo, x_lo_ready)):
                    pe.wait_ge(ready[h], upto(1, i, par, 1))
                    for t in range(CT):
                        last = nc.tensor.matmul(thetaphi_ps[h], tp_w[:, t].rearrange("p a k -> p (a k)"),
                                                part[:, par, t, cols], start=part is x_hi and t == 0,
                                                stop=part is x_lo and t == CT - 1)
                last.then_inc(thetaphi_done, 1)

            def g_projection(i, par, h):
                if h == 0 and (not is_number(i) or i > 0):
                    pe.wait_ge(out_evacuated[1][1], upto(1, i, par, -1))
                elif h == 0 and par == 1:
                    pe.wait_ge(g_pooled, 1)
                if h == 1:
                    pe.wait_ge(thetaphi_summed, upto(2, i, par, 1))
                pe.wait_ge(x_lo_ready[h], upto(1, i, par, 1))
                for t in range(CT):
                    last = three(g_ps[h], (g_hi_w[:, t, :], g_lo_w[:, t, :]), x_parts(par, t, h), t == 0, t == CT - 1)
                last.then_inc(g_done, 1)

            def values(i, par):
                if is_first(i, par):
                    pe.wait_ge(w2_ready, 1)
                else:
                    pe.wait_ge(out_evacuated[0][0], upto(1, i, par, 0))
                pe.wait_ge(g_lo_ready, upto(1, i, par, 1))
                for t in range(MT):
                    tile = slice(t * P, (t + 1) * P)
                    last = three(value_ps[:, t * C:(t + 1) * C], (g_hi[:, tile], g_lo[:, tile]),
                                 (w2_hi[:], w2_lo[:]), True, True)
                last.then_inc(value_done, 1)

            def scores(i, par, h):
                pe.wait_ge(theta_lo_ready, upto(2, i, par, h + 1))
                pe.wait_ge(phi_ready, upto(1, i, par, 1))
                if not is_first(i, par):
                    pe.wait_ge(prob_hi_ready, upto(2, i, par, h - 1))
                tiles = scores_ps[h][:, :, :].rearrange("p a (b m) -> p (a b) m", m=M)
                for t in range(NT):
                    n0 = h * HALF + t * P
                    last = nc.tensor.matmul(tiles[:, t, :], theta_aug[0:R_SHIFT, par, n0:n0 + P],
                                            phi_aug[0:R_SHIFT, par, :], start=True, stop=True)
                last.then_inc(scores_done, 1)

            def shifts_to_rows(i, par):
                pe.wait_ge(shift_parts_ready, upto(1, i, par, 1))
                nc.tensor.matmul(shift_ps, shift_parts[:, :, :].rearrange("p t s -> p (t s)"), ident_r[:],
                                 start=True, stop=True).then_inc(shift_rows_done, 1)

            def scores_transposed(i, par, h):
                pe.wait_ge(shift_rows_ready, upto(2, i, par, h + 1))
                for t in range(MT):
                    last = nc.tensor.matmul(scores_ps[h][:, t, :], phi_aug[0:K_AUG, par, t * P:(t + 1) * P],
                                            theta_aug[0:K_AUG, par, h * HALF:(h + 1) * HALF], start=True, stop=True)
                last.then_inc(scoresT_done, 1)

            def bank(i, par, h, f):
                return (last_out_ps if is_last(i, par) else out_ps)[h][f]

            def filter_x(i, par, h, f):
                if is_first(i, par) and (h, f) == (0, 0):
                    pe.wait_ge(band_parts_ready, 2)
                    pe.wait_ge(edge_w_loaded, EDGE_LOADS)
                if (h, f) == (0, 0):
                    pe.wait_ge(value_lo_ready, upto(1, i, par, 1))
                elif (h, f) == (0, 1):
                    if has_next(i, par):
                        pe.wait_ge(g_pooled, upto(2, *following(i, par), 1))
                    else:
                        pe.wait_ge(out_evacuated[1][1], upto(1, i, par, 0))
                elif (h, f) == (1, 0):
                    if has_next(i, par):
                        pe.wait_ge(thetaphi_summed, upto(2, *following(i, par), 2))
                    else:
                        pe.wait_ge(out_evacuated[1][0], upto(1, i, par, 0))
                elif has_next(i, par):
                    pe.wait_ge(out_evacuated[0][1], upto(1, i, par, 1))
                cols = slice(f * P, (f + 1) * P)
                three(bank(i, par, h, f), (band_hi[:, f, cols], band_lo[:, f, cols]), x_parts(par, f, h), True, False)
                if (h, f) == ((1, 0) if is_last(i, par) else (0, 0)):
                    pe.wait_ge(x_edge_loaded[par], EDGE_LOADS * (i + 1))
                other = 1 - f
                last = nc.tensor.matmul(bank(i, par, h, f), edge_w[:, other * P:(other + 1) * P],
                                        x_edge[:, par, other, h * HALF:(h + 1) * HALF], start=False, stop=False)
                if f == CT - 1:
                    last.then_inc(x_used, 1)

            def add_attention(i, par, h, f, tiles=range(MT)):
                pe.wait_ge(prob_lo_ready, upto(2, i, par, h + 1))
                cols = slice(f * P, (f + 1) * P)
                for t in tiles:
                    last = three(bank(i, par, h, f), (value_hi[:, par, t, cols], value_lo[:, par, t, cols]),
                                 (prob_hi[:, h, t, :], prob_lo[:, h, t, :]), False, t == MT - 1)
                if t == MT - 1:
                    last.then_inc(out_done, 1)

            pe.wait_ge(proj_w_ready, 1)
            for h in range(2):
                theta_phi(0, 0, h)
            pe.wait_ge(g_w_ready, 1)
            g_projection(0, 0, 0)
            pe.wait_ge(o_loaded, 2 * 16)
            pe.wait_ge(band_ready, 1)
            for t in range(CT):
                last = nc.tensor.matmul(w2_ps, o_sb[:, t, :], band[:, t, :], start=t == 0, stop=t == CT - 1)
            last.then_inc(w2_done, 1)
            pe.wait_ge(phi_ones_ready, 1)
            for h in range(2):
                scores(0, 0, h)
            g_projection(0, 0, 1)
            g_projection(0, 1, 0)
            for h in range(2):
                theta_phi(0, 1, h)
            values(0, 0)
            pe.wait_ge(ident_r_ready, 1)
            shifts_to_rows(0, 0)

            def image(i, par):
                ni, npar = following(i, par)
                if is_last(i, par):
                    scores_transposed(i, par, 0)
                    filter_x(i, par, 1, 0)
                    scores_transposed(i, par, 1)
                    filter_x(i, par, 0, 0)
                    filter_x(i, par, 0, 1)
                    filter_x(i, par, 1, 1)
                    for f in range(CT):
                        add_attention(i, par, 0, f)
                    for f in range(CT):
                        add_attention(i, par, 1, f)
                    return
                scores_transposed(i, par, 0)
                if not is_first(i, par):
                    theta_phi(ni, npar, 0)
                scores_transposed(i, par, 1)
                if not is_first(i, par):
                    theta_phi(ni, npar, 1)
                    g_projection(ni, npar, 0)
                filter_x(i, par, 0, 0)
                g_projection(ni, npar, 1)
                filter_x(i, par, 1, 0)
                scores(ni, npar, 0)
                add_attention(i, par, 0, 0, range(0, 1))
                scores(ni, npar, 1)
                add_attention(i, par, 0, 0, range(1, MT))
                filter_x(i, par, 0, 1)
                add_attention(i, par, 0, 1)
                add_attention(i, par, 1, 0)
                values(ni, npar)
                filter_x(i, par, 1, 1)
                shifts_to_rows(ni, npar)
                add_attention(i, par, 1, 1)

            over_images(pe, image)


def kernel(x, L0_conv_theta_w, L0_conv_phi_w, L0_conv_g_w, L0_conv_o_w, L0_conv_gamma, L1_conv_inhibition_filter):
    import numpy as np
    import concourse.bacc as bacc
    from concourse.bass_utils import run_bass_kernel_spmd

    x = np.asarray(x)
    B, C, H, W = x.shape
    arrays = {
        "x": np.ascontiguousarray(x).reshape(B, C, H * W),
        "theta_wT": np.ascontiguousarray(np.asarray(L0_conv_theta_w).T),
        "phi_wT": np.ascontiguousarray(np.asarray(L0_conv_phi_w).T),
        "g_wT": np.ascontiguousarray(np.asarray(L0_conv_g_w).T),
        "o_w": np.ascontiguousarray(np.asarray(L0_conv_o_w)),
        "gamma": np.asarray(L0_conv_gamma).reshape(1),
        "taps": np.asarray(L1_conv_inhibition_filter).reshape(1, -1),
    }
    nc = bacc.Bacc("TRN2", target_bir_lowering=False, num_devices=1)
    aps = [nc.dram_tensor(name, a.shape, mybir.dt.from_np(a.dtype), kind="ExternalInput").ap()
           for name, a in arrays.items()]
    out = nc.dram_tensor("out", (B, C, H * W), F32, kind="ExternalOutput").ap()
    ring = nc.dram_tensor("ring", (1, 2 * C), F32, kind="Internal").ap()
    attention_then_channel_filter(nc, *aps, out, ring)
    got = run_bass_kernel_spmd(nc, [arrays], core_ids=[0])
    return got.results[0]["out"].reshape(B, C, H, W)
```
